# Optimizing a Trainium2 kernel written in Bass

```python
import numpy as np
import jax
import jax.numpy as jnp

def _softmax(x, axis=-1):
    return jax.nn.softmax(x, axis=axis)

def _gelu(x):
    return jax.nn.gelu(x, approximate=True)

def _silu(x):
    return jax.nn.silu(x)

def _sigmoid(x):
    return jax.nn.sigmoid(x)

def _layernorm(x, axis=-1, eps=1e-05):
    m = jnp.mean(x, axis=axis, keepdims=True)
    v = jnp.var(x, axis=axis, keepdims=True)
    return (x - m) / jnp.sqrt(v + eps)

def _scatter_add(tgt, idx, src, axis=0):
    return tgt.at[idx].add(src)

def _segment_sum(src, seg, n):
    return jax.ops.segment_sum(src, seg, n)
kernel_name = 'mk_gnn_preln_d1_gnn_r64_59cb40'

def setup_inputs(seed: int=0):
    np.random.seed(seed)
    _w = jnp.asarray

    def _rec_inputs():
        import jax
        import jax.numpy as jnp
        _gk = jax.random.key(seed)
        x = -0.000202 + 1 * jax.random.normal(jax.random.fold_in(_gk, 1), (100000, 128), jnp.float32)
        src = jax.random.randint(jax.random.fold_in(_gk, 2), (25000,), 0, 100000, jnp.int32)
        dst = jax.random.randint(jax.random.fold_in(_gk, 3), (25000,), 0, 100000, jnp.int32)
        _o = jnp.argsort(dst, stable=True)
        src = src[_o]
        dst = dst[_o]
        edge_attr_128 = -5.16925e-05 + 1.00005 * jax.random.normal(jax.random.fold_in(_gk, 11), (25000, 128), jnp.float32)
        return (x, src, dst, edge_attr_128)
    x, src, dst, edge_attr_128 = _rec_inputs()

    def _L0_gnn_setup():
        import jax, jax.numpy as jnp
        import numpy as np
        N_NODES = 50000
        N_EDGES = 12500
        D = 128
        key = jax.random.key(seed)
        ks = jax.random.split(key, 7)
        x = jax.random.normal(ks[0], (N_NODES, D), dtype=jnp.float32)
        edge_index = jax.random.randint(ks[1], (2, N_EDGES), 0, N_NODES, dtype=jnp.int32)
        edge_attr = jax.random.normal(ks[2], (N_EDGES, D), dtype=jnp.float32)
        W1 = jax.random.normal(ks[3], (D, D), dtype=jnp.float32) / np.sqrt(D)
        b1 = jnp.zeros((D,), dtype=jnp.float32)
        W2 = jax.random.normal(ks[4], (D, D), dtype=jnp.float32) / np.sqrt(D)
        b2 = jnp.zeros((D,), dtype=jnp.float32)
        eps = jnp.zeros((), dtype=jnp.float32)
        return {'x': x, 'edge_index': edge_index, 'edge_attr': edge_attr, 'W1': W1, 'b1': b1, 'W2': W2, 'b2': b2, 'eps': eps}
    _L0_gnn_all = _L0_gnn_setup()
    _L0_gnn_in = {k: v for k, v in _L0_gnn_all.items() if k in ('W1', 'b1', 'W2', 'b2', 'eps')}
    del _L0_gnn_all
    return {'x': x, 'src': src, 'dst': dst, 'edge_attr_128': edge_attr_128, 'L0_gnn_W1': _L0_gnn_in['W1'], 'L0_gnn_b1': _L0_gnn_in['b1'], 'L0_gnn_W2': _L0_gnn_in['W2'], 'L0_gnn_b2': _L0_gnn_in['b2'], 'L0_gnn_eps': _L0_gnn_in['eps']}

def reference(x, src, dst, edge_attr_128, L0_gnn_W1, L0_gnn_b1, L0_gnn_W2, L0_gnn_b2, L0_gnn_eps):
    import jax
    import jax.numpy as jnp

    def _L0_gnn_ref(x, edge_index, edge_attr, W1, b1, W2, b2, eps):
        import jax, jax.numpy as jnp
        import numpy as np
        N_NODES = 50000
        N_EDGES = 12500
        D = 128
        src = edge_index[0]
        dst = edge_index[1]
        msg = jax.nn.relu(x[src] + edge_attr)
        agg = jax.ops.segment_sum(msg, dst, num_segments=x.shape[0])
        h = (1.0 + eps) * x + agg
        h = jax.nn.relu(h @ W1 + b1)
        return h @ W2 + b2
    edge_index = jnp.stack([src, dst])
    h = jnp.maximum(_layernorm(x, axis=-1), 0.0)
    x = x + _L0_gnn_ref(h, edge_index, edge_attr_128, L0_gnn_W1, L0_gnn_b1, L0_gnn_W2, L0_gnn_b2, L0_gnn_eps)
    return x

_drawn_inputs = setup_inputs


def setup_inputs(seed=0):
    import zlib

    import numpy as np

    out = dict(_drawn_inputs(seed))
    spreads = {'L0_gnn_b1': (0.0, 0.1), 'L0_gnn_b2': (0.0, 0.1)}
    factors = {}
    for name, (base, spread) in spreads.items():
        noise = np.random.default_rng([zlib.crc32(name.encode()), seed]).standard_normal(out[name].shape)
        drawn = base * np.exp(spread * noise) if base else spread * noise
        out[name] = jnp.asarray(drawn.astype(out[name].dtype))
    for name, factor in factors.items():
        out[name] = (out[name] * factor).astype(out[name].dtype)
    return out
```

```python
import concourse.bass as bass
from concourse import mybir
from contextlib import ExitStack

NODES = 100000
EDGES = 25000
D = 128
LN_EPS = 1e-5

TILES = 4
BLOCK = 128 * TILES
N_BLOCKS = -(-NODES // BLOCK)
LAST = N_BLOCKS - 1
LAST_BASE = NODES - BLOCK
LAST_P0 = (LAST * BLOCK - LAST_BASE) // TILES
WINS = 2
WNODES = BLOCK // WINS
WP = 128 // WINS
WIN_EDGES = 128
STARTS = 512
EP, EC = 125, 200
U = 20
H_SLOTS = 10
GE = 125
G_ROUNDS = EDGES // GE
ZERO = 10240
ZERO_DMAS = NODES // 125 * D // ZERO
G_STEPS = 10
G_DENSE = 4
BATCH = 4
NORM_LAG = 5
SUM_LAG = 6
HIGH_LAG = 7
LOW_LAG = 8
PE_LAG = 9
COPY_LAG = 10
UP_LAG = 11
RELU_LAG = 12
DOWN_LAG = 13
ADD_LAG = 14
STORE_LAG = 16
WIN_LEAD = 4
EDGE_LAG = 8


def gnn_layer(nc, x, pairs, dst_flat, edge_attr, w1, b1, w2, b2, eps, out):
    fp32 = mybir.dt.float32
    fp32r = mybir.dt.float32r
    bf16 = mybir.dt.bfloat16
    i32 = mybir.dt.int32
    ALU = mybir.AluOpType
    ACT = mybir.ActivationFunctionType
    AX = mybir.AxisListType

    agg = nc.dram_tensor("agg", (NODES, D), fp32).ap()

    ctx = ExitStack()
    with ctx:
        def sb(name, shape, dt):
            return ctx.enter_context(nc.sbuf_tensor(name, shape, dt))

        def pb(name, shape, dt):
            return ctx.enter_context(nc.psum_tensor(name, shape, dt))

        def sem(name):
            return ctx.enter_context(nc.semaphore(name))

        x_t = sb("x_t", [128, U, TILES, D], fp32)
        pair_t = sb("pair_t", [128, U, WINS, 2], i32)
        ea_t = sb("ea_t", [128, U, WINS, D], fp32)
        xs_t = sb("xs_t", [128, U, WINS, D], fp32)
        h_t = sb("h_t", [128, H_SLOTS, TILES, D], fp32)
        z_t = sb("z_t", [128, H_SLOTS, WINS, D], fp32)
        m_hi = sb("m_hi", [128, 4, WINS, D], fp32r)
        m_lo = sb("m_lo", [128, 4, WINS, D], fp32r)
        sel = sb("sel", [128, 4, WINS, TILES, WP], fp32r)
        rel = sb("rel", [128, 4, WINS], fp32)
        hT = sb("hT", [128, 4, BLOCK], fp32)
        uT = sb("uT", [128, 4, BLOCK], fp32)
        o_t = sb("o_t", [128, 4, TILES, D], fp32)
        NS = BATCH * (TILES + WINS)
        stats = sb("stats", [128, U // BATCH, NS, 3], fp32)
        std = sb("std", [128, U // BATCH, NS], fp32)
        rstd = sb("rstd", [128, U // BATCH, NS], fp32)
        nbias = sb("nbias", [128, U // BATCH, NS], fp32)
        ident = sb("ident", [128, 128], fp32)
        ones = sb("ones", [128, 128], fp32)
        w1_sb = sb("w1_sb", [D, D], fp32)
        w1s = sb("w1s", [D, D], fp32)
        w2_sb = sb("w2_sb", [D, D], fp32)
        b1_sb = sb("b1_sb", [D, 1], fp32)
        b2_sb = sb("b2_sb", [128, 3, D], fp32)
        b2_part = sb("b2_part", [128, 2, D], bf16)
        b2_rows = sb("b2_rows", [128, TILES, D], bf16)
        b2_ones = sb("b2_ones", [128, 128], bf16)
        eps_sb = sb("eps_sb", [128, 1], fp32)
        scale_sb = sb("scale_sb", [128, 4], fp32)
        lneps = sb("lneps", [128, 1], fp32)
        offs = sb("offs", [128, TILES, WP], fp32)
        base = sb("base", [128, U, WINS], fp32)
        dst_i = sb("dst_i", [EP, EC], i32)
        dst_f = sb("dst_f", [EP, EC], fp32)
        prev_i = sb("prev_i", [128, 1], i32)
        prev_f = sb("prev_f", [128, 1], fp32)
        t_row = sb("t_row", [EP, STARTS], fp32)
        t_col = sb("t_col", [128, 4], fp32)
        below = sb("below", [EP, STARTS], fp32)
        cut = sb("cut", [EP, STARTS], fp32)
        e_c = sb("e_c", [EP, 1], fp32)
        junk = sb("junk", [128, EC], fp32)
        cnt = sb("cnt", [128, 4], fp32)
        pos = sb("pos", [128, 4], fp32)
        viol = sb("viol", [EP, EC], fp32)
        viols = sb("viols", [EP, 1], fp32)
        row = sb("row", [1, STARTS], fp32)
        gap = sb("gap", [1, STARTS], fp32)
        low = sb("low", [1, 4], fp32)
        starts = sb("starts", [1, STARTS], i32)
        flag = sb("flag", [1, 1], i32)

        ps_h = [pb(f"ps_h{i}", [128, BLOCK], fp32) for i in range(2)]
        ps_u = [pb(f"ps_u{i}", [128, BLOCK], fp32) for i in range(2)]
        ps_o = [pb(f"ps_o{i}", [128, BLOCK], fp32) for i in range(2)]
        ps_a = pb("ps_a", [128, 512], fp32)
        ps_b = pb("ps_b", [128, 512], fp32)

        s_dst = sem("dst_loaded")
        s_prm = sem("params_loaded")
        s_pool = sem("pool_constants")
        s_dve = sem("dve_chain")
        pairs_seen = sem("pairs_seen")
        scales_seen = sem("scales_seen")
        s_der = sem("derived_params_ready")
        s_cut = sem("cuts_ready")
        s_rows = sem("cut_rows_ready")
        s_pos = sem("positions_ready")
        s_posT = sem("positions_row_ready")
        s_flag = sem("starts_and_flag_ready")
        x_loaded = [sem(f"x_loaded{i}") for i in range(U // 2)]
        pair_loaded = [sem(f"pair_loaded{i}") for i in range(U)]
        ea_loaded = [sem(f"ea_loaded{i}") for i in range(U)]
        xs_gathered = [sem(f"xs_gathered{i}") for i in range(U)]
        stored = [sem(f"stored{i}") for i in range(2)]
        stats_ready = sem("stats_ready")
        std_ready = sem("std_ready")
        rstd_ready = sem("rstd_ready")
        scales_ready = sem("scales_ready")
        h_ready = sem("h_ready")
        z_ready = sem("z_ready")
        v_ready = sem("v_ready")
        hi_ready = sem("hi_ready")
        lo_ready = sem("lo_ready")
        rel_ready = sem("rel_ready")
        base_ready = sem("base_ready")
        sel_ready = sem("sel_ready")
        psh_ready = sem("psh_ready")
        hT_ready = sem("hT_ready")
        psu_ready = sem("psu_ready")
        uT_ready = sem("uT_ready")
        pso_ready = sem("pso_ready")
        o_ready = sem("o_ready")

        g_stats = sb("g_stats", [128, TILES, 6], fp32)
        g_mv = sb("g_mv", [128, TILES, 2], fp32)
        g_sd = sb("g_sd", [128, TILES], fp32)
        g_rstd = sb("g_rstd", [128, TILES], fp32)
        g_any_t = sb("g_any_t", [128, 2], fp32)
        g_idx_t = sb("g_idx_t", [128, 1], i32)
        t_idx = sb("t_idx", [128, 1], fp32)
        g_col_t = sb("g_col_t", [128, 128], fp32)
        g_idx, g_any, g_dst = g_idx_t[0:GE, :], g_any_t[0:GE, 0:1], g_any_t[0:GE, 1:2]
        g_col = g_col_t[0:GE, 0:GE]
        g_row_i = t_row[0:GE, 0:GE].bitcast(i32)
        g_row, g_same = below[0:GE, 0:GE], below[0:GE, 128:128 + GE]
        g_dup, g_before = below[0:GE, 256:256 + GE], cut[0:GE, 0:GE]
        agg_flat = agg.rearrange("(p n) f -> p (n f)", p=125)
        zeros = x_t[0:125, :, :, :].rearrange("p u j f -> p (u j f)")[:, 0:ZERO]
        g_zeroed = sem("g_zeroed")
        g_zeros, g_agg, g_in, g_xs, g_dve = (sem("g_" + k) for k in ("zeros", "agg", "in", "xs", "dve"))
        g_var, g_std, g_msg, g_psum, g_sum = (sem("g_" + k) for k in ("var", "std", "msg", "psum", "sum"))
        g_x, g_h, g_psh, g_hT, g_psu, g_uT = (sem("g_" + k) for k in ("x", "h", "psh", "hT", "psu", "uT"))
        g_pso, g_o, g_stored, g_free = (sem("g_" + k) for k in ("pso", "o", "stored", "free"))

        block = ctx.enter_context(nc.Block())

        def cut_psum(q):
            return (ps_h + ps_u)[q]

        def ordinary(eng):
            eng.wait_ge(s_flag, 1)
            return eng.value_load(flag[0:1, 0:1], min_val=0, max_val=2)

        def pipeline(eng, step, lag):
            for c in range(U):
                step(0, c)
            with eng.Fori(1, N_BLOCKS // U) as i:
                for c in range(U):
                    step(i, c)
            for n in range(N_BLOCKS // U * U, N_BLOCKS + lag):
                step(n // U, n % U)

        def run(stage, i, c, lag=0):
            i, c = i + (c - lag) // U, (c - lag) % U
            if not isinstance(i, int) or 0 <= i * U + c < N_BLOCKS:
                stage(i, c)

        def is_last(i, c):
            return isinstance(i, int) and i * U + c == LAST

        def no(i, c):
            return i * U + c

        def at_least(eng, sem, value):
            if not isinstance(value, int) or value > 0:
                eng.wait_ge(sem, value)

        @block.sync
        def _(sp):
            nc.sync.dma_start(dst_i[:], dst_flat.rearrange("(p c) -> p c", c=EC)).then_inc(s_dst, 16)
            sp.wait_ge(s_pool, 1)
            with nc.allow_non_contiguous_dma(reason="124 elements once"):
                nc.sync.dma_start(prev_i[1:EP, :], dst_flat.rearrange("(p c) -> p c", c=EC)[0:EP - 1, EC - 1:EC]
                                  ).then_inc(s_dst, 16)
            nc.sync.dma_start(w1_sb[:], w1).then_inc(s_prm, 16)
            nc.sync.dma_start(w2_sb[:], w2).then_inc(s_prm, 16)
            nc.sync.dma_start(b1_sb[:], b1.rearrange("(p o) -> p o", o=1)).then_inc(s_prm, 16)
            nc.sync.dma_start(b2_sb[:, 0, :], b2.rearrange("(o f) -> o f", o=1).to_broadcast([128, D])
                              ).then_inc(s_prm, 16)
            nc.sync.dma_start(eps_sb[:], eps.rearrange("(o f) -> o f", o=1).to_broadcast([128, 1])
                              ).then_inc(s_prm, 16)

            def load_x(i, c):
                at_least(sp, o_ready, no(i, c) - U + 2)
                if isinstance(i, int) and no(i, c) == LAST - 1:
                    for b, first in ((0, no(i, c) * BLOCK), (1, LAST_BASE)):
                        sp.dma_start(x_t[:, c + b, :, :], x[first:first + BLOCK, :].rearrange("(p j) f -> p j f", j=TILES)
                                      ).then_inc(x_loaded[c // 2], 16)
                else:
                    sp.dma_start(x_t[:, c:c + 2, :, :].rearrange("p b j f -> p b (j f)"),
                                  x[bass.ds(no(i, c) * BLOCK, 2 * BLOCK), :].rearrange("(b p j) f -> p b (j f)", b=2, j=TILES)
                                  ).then_inc(x_loaded[c // 2], 16)

            start_regs = [sp.alloc_register(f"window_start{w}") for w in range(WINS)]

            def load_windows(i, c):
                if isinstance(i, int) and no(i, c) == 0:
                    sp.wait_ge(s_flag, 1)
                at_least(sp, rel_ready, no(i, c) - U + 1)
                sp.load(start_regs, starts[0:1, bass.ds(no(i, c) * WINS, WINS)])
                for w in range(WINS):
                    s = sp.snap(start_regs[w], min_val=0, max_val=EDGES - WIN_EDGES)
                    sp.dma_start(pair_t[:, c, w, :], pairs[bass.ds(s, WIN_EDGES), :]).then_inc(pair_loaded[c], 16)
                    sp.dma_start(ea_t[:, c, w, :], edge_attr[bass.ds(s, WIN_EDGES), :]).then_inc(ea_loaded[c], 16)

            def step(i, c):
                if c % 2 == 0:
                    run(load_x, i, c)
                if isinstance(i, int) and no(i, c) == 0:
                    for k in range(WIN_LEAD):
                        load_windows(0, k)
                run(load_windows, i, c, -WIN_LEAD)

            def in_any_order():
                sp.wait_ge(g_zeros, 1)
                for k in range(ZERO_DMAS):
                    sp.dma_start(agg_flat[:, k * ZERO:k * ZERO + ZERO], zeros).then_inc(g_zeroed, 16)
                sp.wait_ge(g_zeroed, 16 * ZERO_DMAS)

                def load_round(t):
                    rows = bass.ds(t * GE, GE)
                    sp.dma_start(pair_t[0:GE, 0, 0, :], pairs[rows, :]).then_inc(g_in, 16)
                    sp.dma_start(ea_t[0:GE, 0, 0, :], edge_attr[rows, :]).then_inc(g_in, 16)
                    sp.dma_start(g_row_i, dst_flat[rows].rearrange("(o e) -> o e", o=1).to_broadcast([GE, GE])
                                 ).then_inc(g_in, 16)

                load_round(0)
                with sp.Fori(1, G_ROUNDS) as t:
                    sp.wait_ge(g_agg, 16 * t)
                    sp.sem_inc(g_free, 1)
                    load_round(t)
                sp.wait_ge(g_agg, 16 * G_ROUNDS)

                def dense(n):
                    first = LAST_BASE if n is LAST else n * BLOCK
                    p0 = LAST_P0 if n is LAST else 0
                    rows = bass.ds(first, BLOCK)
                    sp.dma_start(x_t[:, 0, :, :], x[rows, :].rearrange("(p j) f -> p j f", j=TILES)).then_inc(g_x, 16)
                    sp.dma_start(x_t[:, 1, :, :], agg[rows, :].rearrange("(p j) f -> p j f", j=TILES)).then_inc(g_x, 16)
                    sp.wait_ge(g_o, n + 1)
                    sp.dma_start(out[bass.ds(n * BLOCK, BLOCK - TILES * p0), :].rearrange("(p j) f -> p (j f)", j=TILES),
                                 o_t[p0:128, 0, :, :].rearrange("p j f -> p (j f)")).then_inc(g_stored, 16)
                    sp.wait_ge(g_stored, 16 * n + 16)
                    sp.sem_inc(g_free, 1)

                with sp.Fori(0, LAST) as n:
                    dense(n)
                dense(LAST)

            with sp.If(ordinary(sp) == 0):
                pipeline(sp, step, 0)
            with sp.Else():
                in_any_order()

        @block.gpsimd
        def _(pool):
            nc.gpsimd.memset(prev_i[:], -1).then_inc(s_pool, 1)
            nc.gpsimd.iota(t_row[:], [[WNODES, STARTS]], base=0, channel_multiplier=0,
                           allow_small_or_imprecise_dtypes=True)
            nc.gpsimd.iota(t_col[:], [[128, 4]], base=0, channel_multiplier=1,
                           allow_small_or_imprecise_dtypes=True)
            nc.gpsimd.iota(offs[:], [[1, TILES], [TILES, WP]], base=0, channel_multiplier=0,
                           allow_small_or_imprecise_dtypes=True)
            nc.gpsimd.iota(base[:], [[WNODES, U * WINS]], base=0, channel_multiplier=0,
                           allow_small_or_imprecise_dtypes=True)
            nc.gpsimd.iota(t_idx[:], [[0, 1]], base=0, channel_multiplier=1,
                           allow_small_or_imprecise_dtypes=True)
            nc.gpsimd.iota(g_col_t[:], [[1, 128]], base=0, channel_multiplier=0,
                           allow_small_or_imprecise_dtypes=True)
            nc.gpsimd.memset(ones[:], 1.0)
            nc.gpsimd.memset(e_c[:], float(EC))
            nc.gpsimd.memset(b2_rows[:], 0.0)
            nc.gpsimd.memset(b2_ones[:], 0.0)
            nc.gpsimd.memset(lneps[:], LN_EPS).then_inc(s_pool, 1)
            pool.wait_ge(s_pool, 2)
            nc.gpsimd.affine_select(out=ident[:], in_=ones[:], compare_op=ALU.is_equal, fill=0.0, base=0,
                                    pattern=[[-1, 128]], channel_multiplier=1).then_inc(s_pool, 1)

            def gather(i, c):
                pool.wait_ge(pair_loaded[c], 16 * WINS * (i + 1))
                pool.sem_inc(pairs_seen, 1)
                for w in range(WINS):
                    pool.indirect_dma_start(
                        out=xs_t[:, c, w, :], out_offset=None, in_=x,
                        in_offset=bass.IndirectOffsetOnAxis(ap=pair_t[:, c, w, 0:1], axis=0),
                    ).then_inc(xs_gathered[c], 16)

            def normalise_edges(i, c):
                k = c // BATCH
                at_least(pool, lo_ready, no(i, c) - H_SLOTS + 1)
                pool.wait_ge(scales_ready, i * (U // BATCH) + k + 1)
                pool.sem_inc(scales_seen, 1)
                for w in range(WINS):
                    q = c % BATCH * (TILES + WINS) + TILES + w
                    last = nc.gpsimd.tensor_scalar(z_t[:, c % H_SLOTS, w, :], xs_t[:, c, w, :], rstd[:, k, q:q + 1],
                                                   nbias[:, k, q:q + 1], ALU.mult, ALU.add)
                last.then_inc(z_ready, 1)

            def step(i, c):
                run(gather, i, c)
                run(normalise_edges, i, c, EDGE_LAG)

            def in_any_order():
                with pool.Fori(0, G_ROUNDS) as t:
                    pool.wait_ge(g_in, 48 * t + 48)
                    pool.sem_inc(pairs_seen, 1)
                    pool.indirect_dma_start(
                        out=xs_t[0:GE, 0, 0, :], out_offset=None, in_=x,
                        in_offset=bass.IndirectOffsetOnAxis(ap=pair_t[0:GE, 0, 0, 0:1], axis=0)).then_inc(g_xs, 16)
                    pool.indirect_dma_start(
                        out=xs_t[0:GE, 0, 1, :], out_offset=None, in_=agg,
                        in_offset=bass.IndirectOffsetOnAxis(ap=pair_t[0:GE, 0, 0, 1:2], axis=0)).then_inc(g_xs, 16)
                    pool.wait_ge(g_sum, t + 1)
                    pool.sem_inc(scales_seen, 1)
                    pool.indirect_dma_start(
                        out=agg, out_offset=bass.IndirectOffsetOnAxis(ap=g_idx, axis=0), in_=xs_t[0:GE, 0, 1, :],
                        in_offset=None, bounds_check=NODES - 1, oob_is_err=False).then_inc(g_agg, 16)

            with pool.If(ordinary(pool) == 0):
                pipeline(pool, step, EDGE_LAG)
            with pool.Else():
                in_any_order()

        @block.vector
        def _(dve):
            ve = nc.vector
            chain = [0]

            def link(ins):
                chain[0] += 1
                ins.then_inc(s_dve, 1)
                dve.wait_ge(s_dve, chain[0])

            dve.wait_ge(s_dst, 32)
            ve.tensor_copy(prev_f[:], prev_i[:])
            link(ve.tensor_copy(dst_f[:], dst_i[:]))
            dve.wait_ge(s_pool, 3)
            link(ve.tensor_scalar(t_col[:], t_col[:], float(WNODES), None, ALU.mult))
            ve.tensor_scalar(below[:], t_row[:], dst_f[:, EC - 1:EC], None, ALU.is_gt)
            link(ve.tensor_scalar(cut[:], t_row[:], prev_f[0:EP, :], None, ALU.is_gt))
            ve.tensor_tensor(cut[:], cut[:], below[:], ALU.subtract).then_inc(s_cut, 1)
            ve.tensor_tensor(viol[:, 1:EC], dst_f[:, 1:EC], dst_f[:, 0:EC - 1], ALU.is_lt)
            link(ve.tensor_tensor(viol[:, 0:1], dst_f[:, 0:1], prev_f[0:EP, :], ALU.is_lt))
            ve.tensor_reduce(viols[:], viol[:], AX.X, ALU.add).then_inc(s_cut, 1)
            dve.wait_ge(s_rows, 1)
            for q in range(4):
                last = ve.tensor_scalar(junk[:], cut_psum(q)[:, 0:EC], t_col[:, q:q + 1], None, ALU.is_lt)
                link(last)
                link(ve.tensor_reduce(cnt[:, q:q + 1], junk[:], AX.X, ALU.add))
                last = ve.tensor_tensor(pos[:, q:q + 1], cnt[:, q:q + 1], cut_psum(q)[:, EC:EC + 1], ALU.add)
            last.then_inc(s_pos, 1)
            dve.wait_ge(s_posT, 1)
            link(ve.tensor_scalar(row[:], ps_a[0:1, 0:STARTS], float(EDGES), None, ALU.min))
            ve.tensor_scalar(starts[:], row[:], float(EDGES - WIN_EDGES), None, ALU.min)
            link(ve.tensor_tensor(gap[:, 0:STARTS - 1], row[:, 1:STARTS], row[:, 0:STARTS - 1], ALU.subtract))
            ve.tensor_scalar(low[:, 1:2], ps_b[0:1, 0:1], 0.5, None, ALU.is_gt)
            link(ve.tensor_reduce(low[:, 0:1], gap[:, 0:STARTS - 1], AX.X, ALU.max))
            link(ve.tensor_scalar(low[:, 2:3], low[:, 0:1], WIN_EDGES + 0.5, None, ALU.is_gt))
            ve.tensor_tensor(flag[:], low[:, 2:3], low[:, 1:2], ALU.add).then_inc(s_flag, 1)

            dve.wait_ge(s_prm, 80)
            link(ve.tensor_scalar(scale_sb[:, 0:1], eps_sb[:], 1.0, None, ALU.add))
            link(ve.tensor_scalar(scale_sb[:, 1:2], scale_sb[:, 0:1], -1.0, None, ALU.mult))
            ve.tensor_tensor(scale_sb[:, 2:3], scale_sb[:, 0:1], scale_sb[:, 1:2], ALU.max)
            link(ve.tensor_scalar(scale_sb[:, 3:4], scale_sb[:, 0:1], 0.0, 2.0, ALU.is_ge, ALU.mult))
            link(ve.tensor_scalar(scale_sb[:, 3:4], scale_sb[:, 3:4], -1.0, None, ALU.add))
            ve.tensor_scalar(w1s[:], w1_sb[:], scale_sb[:, 3:4], None, ALU.mult)
            link(ve.tensor_copy(b2_part[:, 0, :], b2_sb[:, 0, :]))
            link(ve.tensor_tensor(b2_sb[:, 1, :], b2_sb[:, 0, :], b2_part[:, 0, :], ALU.subtract))
            link(ve.tensor_copy(b2_part[:, 1, :], b2_sb[:, 1, :]))
            link(ve.tensor_tensor(b2_sb[:, 2, :], b2_sb[:, 1, :], b2_part[:, 1, :], ALU.subtract))
            for r, part in ((0, 0), (32, 1), (64, 2)):
                ve.memset(b2_ones[r:r + 1, :], 1.0)
                for j in range(TILES):
                    last = ve.tensor_copy(b2_rows[r:r + 1, j, :], b2_sb[r:r + 1, part, :])
            last.then_inc(s_der, 1)

            def rows_stats(i, c):
                k = c // BATCH
                o = (c % BATCH) * (TILES + WINS)
                dve.wait_ge(x_loaded[c // 2], 16 * (i + (2 if isinstance(i, int) and no(i, c) >= LAST - 1 else 1)))
                for j in range(0, TILES, 2):
                    ve.bn_stats(stats[:, k, o + j:o + j + 2, :].rearrange("p a b -> p (a b)"),
                                x_t[:, c, j:j + 2, :].rearrange("p j f -> p f j"))
                dve.wait_ge(xs_gathered[c], 16 * WINS * (i + 1))
                last = ve.bn_stats(stats[:, k, o + TILES:o + TILES + WINS, :].rearrange("p a b -> p (a b)"),
                                   xs_t[:, c, :, :].rearrange("p j f -> p f j"))
                if c % BATCH == BATCH - 1:
                    last.then_inc(stats_ready, 1)

            def scales(i, c):
                k = c // BATCH
                q = i * (U // BATCH) + k + 1
                dve.wait_ge(std_ready, q)
                ve.reciprocal(rstd[:, k, :], std[:, k, :]).then_inc(rstd_ready, 1)
                dve.wait_ge(rstd_ready, 2 * q - 1)
                rn = rstd[:, k, :].rearrange("p (b r) -> p b r", b=BATCH)[:, :, 0:TILES]
                ve.tensor_scalar(rn, rn, scale_sb[:, 2:3], None, ALU.mult).then_inc(rstd_ready, 1)
                dve.wait_ge(rstd_ready, 2 * q)
                ve.scalar_tensor_tensor(out=nbias[:, k, :], in0=stats[:, k, :, 1], scalar=-1.0, in1=rstd[:, k, :],
                                        op0=ALU.mult, op1=ALU.mult).then_inc(scales_ready, 1)

            def edge_sum(i, c):
                dve.wait_ge(z_ready, no(i, c) + 1)
                dve.wait_ge(ea_loaded[c], 16 * WINS * (i + 1))
                ve.scalar_tensor_tensor(out=z_t[:, c % H_SLOTS, :, :], in0=z_t[:, c % H_SLOTS, :, :], scalar=0.0, in1=ea_t[:, c, :, :],
                                        op0=ALU.max, op1=ALU.add).then_inc(v_ready, 1)

            def edge_low(i, c):
                s = c % 4
                dve.wait_ge(hi_ready, no(i, c) + 1)
                ve.scalar_tensor_tensor(out=m_lo[:, s, :, :], in0=z_t[:, c % H_SLOTS, :, :], scalar=0.0,
                                        in1=m_hi[:, s, :, :].bitcast(fp32),
                                        op0=ALU.max, op1=ALU.subtract).then_inc(lo_ready, 1)

            def relative(i, c):
                s = c % 4
                if is_last(i, c):
                    for w in range(WINS):
                        last = ve.tensor_scalar(rel[:, s, w:w + 1], pair_t[:, c, w, 1:2],
                                                -float(LAST_BASE + w * WNODES), None, ALU.add)
                    last.then_inc(rel_ready, 1)
                    return
                if c == 0 and not (isinstance(i, int) and i == 0):
                    dve.wait_ge(rel_ready, no(i, c))
                    ve.tensor_scalar(base[:], base[:], float(U * BLOCK), None, ALU.add).then_inc(base_ready, 1)
                    dve.wait_ge(base_ready, i)
                ve.tensor_tensor(rel[:, s, :], pair_t[:, c, :, 1], base[:, c, :], ALU.subtract).then_inc(rel_ready, 1)

            def select(i, c):
                s = c % 4
                dve.wait_ge(rel_ready, no(i, c) + 1)
                at_least(dve, psh_ready, no(i, c) - 3)
                for w in range(WINS):
                    last = ve.tensor_scalar(sel[:, s, w, :, :], offs[:], rel[:, s, w:w + 1], scale_sb[:, 3:4],
                                            ALU.is_equal, ALU.mult)
                last.then_inc(sel_ready, 1)

            def add(i, c):
                s = c % 4
                dve.wait_ge(pso_ready, no(i, c) + 1)
                at_least(dve, stored[s // 2], 16 * (i * (U // 4) + c // 4))
                ve.tensor_tensor(o_t[:, s, :, :].rearrange("p j f -> p (j f)"), ps_o[c % 2][:],
                                 x_t[:, c, :, :].rearrange("p j f -> p (j f)"), ALU.add).then_inc(o_ready, 1)

            def step(i, c):
                run(rows_stats, i, c)
                run(add, i, c, ADD_LAG)
                if c % BATCH == 0:
                    run(scales, i, c, 1)
                run(select, i, c, LOW_LAG)
                run(edge_low, i, c, LOW_LAG)
                run(edge_sum, i, c, SUM_LAG)
                run(relative, i, c, SUM_LAG)

            def in_any_order():
                ve.memset(zeros, 0.0).then_inc(g_zeros, 1)
                ve.tensor_scalar(g_before, g_col, t_idx[0:GE, :], None, ALU.is_lt)

                with dve.Fori(0, G_ROUNDS) as t:
                    step_no = [0]

                    def then(ins):
                        step_no[0] += 1
                        ins.then_inc(g_dve, 1)
                        dve.wait_ge(g_dve, t * G_STEPS + step_no[0])

                    xs, ag, msg = xs_t[0:GE, 0, 0, :], xs_t[0:GE, 0, 1, :], z_t[0:GE, 0, 0, :]
                    st, mv = g_stats[0:GE, 0, :], g_mv[0:GE, 0, :]
                    dve.wait_ge(g_xs, 32 * t + 32)
                    then(ve.bn_stats(st, xs))
                    ve.tensor_copy(g_dst, pair_t[0:GE, 0, 0, 1:2])
                    ve.bn_aggr(mv, st).then_inc(g_var, 1)
                    dve.wait_ge(g_std, t + 1)
                    then(ve.reciprocal(g_rstd[0:GE, 0:1], g_sd[0:GE, 0:1]))
                    then(ve.tensor_scalar(msg, xs, mv[:, 0:1], g_rstd[0:GE, 0:1], ALU.subtract, ALU.mult))
                    then(ve.scalar_tensor_tensor(out=msg, in0=msg, scalar=0.0, in1=ea_t[0:GE, 0, 0, :],
                                                 op0=ALU.max, op1=ALU.add))
                    then(ve.tensor_scalar(msg, msg, 0.0, None, ALU.max))
                    then(ve.tensor_copy(g_row, g_row_i))
                    ve.tensor_scalar(g_same, g_row, g_dst, None, ALU.is_equal).then_inc(g_msg, 1)
                    dve.wait_ge(g_msg, t + 1)
                    then(ve.tensor_tensor(g_dup, g_same, g_before, ALU.mult))
                    then(ve.tensor_reduce(g_any, g_dup, AX.X, ALU.max))
                    then(ve.tensor_scalar(g_any, g_any, float(1 << 20), None, ALU.mult))
                    then(ve.tensor_tensor(g_idx, g_any, g_dst, ALU.add))
                    dve.wait_ge(g_psum, t + 1)
                    ve.tensor_tensor(ag, ps_a[0:GE, 0:D], ag, ALU.add).then_inc(g_sum, 1)
                    assert step_no[0] == G_STEPS

                def dense(n):
                    step_no = [0]

                    def then(ins):
                        step_no[0] += 1
                        ins.then_inc(g_dve, 1)
                        dve.wait_ge(g_dve, G_ROUNDS * G_STEPS + n * G_DENSE + step_no[0])

                    dve.wait_ge(g_x, 32 * n + 32)
                    for j in range(TILES):
                        last = ve.bn_stats(g_stats[:, j, :], x_t[:, 0, j, :])
                    then(last)
                    ve.tensor_copy(g_any_t[:, 0:1], t_idx[:])
                    for j in range(TILES):
                        last = ve.bn_aggr(g_mv[:, j, :], g_stats[:, j, :])
                    last.then_inc(g_var, 1)
                    dve.wait_ge(g_std, G_ROUNDS + n + 1)
                    then(ve.reciprocal(g_rstd[:], g_sd[:]))
                    for j in range(TILES):
                        last = ve.tensor_scalar(h_t[:, 0, j, :], x_t[:, 0, j, :], g_mv[:, j, 0:1], g_rstd[:, j:j + 1],
                                                ALU.subtract, ALU.mult)
                    then(last)
                    then(ve.tensor_scalar(h_t[:, 0, :, :], h_t[:, 0, :, :], 0.0, scale_sb[:, 0:1], ALU.max, ALU.mult))
                    ve.tensor_tensor(h_t[:, 0, :, :], h_t[:, 0, :, :], x_t[:, 1, :, :], ALU.add).then_inc(g_h, 1)
                    dve.wait_ge(g_pso, n + 1)
                    ve.tensor_tensor(o_t[:, 0, :, :].rearrange("p j f -> p (j f)"), ps_o[0][:],
                                     x_t[:, 0, :, :].rearrange("p j f -> p (j f)"), ALU.add).then_inc(g_o, 1)
                    assert step_no[0] == G_DENSE

                with dve.Fori(0, LAST) as n:
                    dense(n)
                dense(LAST)

            with dve.If(ordinary(dve) == 0):
                pipeline(dve, step, ADD_LAG)
            with dve.Else():
                in_any_order()

        @block.scalar
        def _(act):
            sc = nc.scalar

            def store(i, c):
                k = c % 4 // 2
                act.wait_ge(o_ready, no(i, c) + 2)
                if isinstance(i, int) and no(i, c) == LAST - 1:
                    act.dma_start(out[(LAST - 1) * BLOCK:LAST * BLOCK, :].rearrange("(p j) f -> p (j f)", j=TILES),
                                  o_t[:, 2 * k, :, :].rearrange("p j f -> p (j f)")).then_inc(stored[k], 16)
                    act.dma_start(out[LAST * BLOCK:NODES, :].rearrange("(p j) f -> p (j f)", j=TILES),
                                  o_t[LAST_P0:128, 2 * k + 1, :, :].rearrange("p j f -> p (j f)")).then_inc(stored[k], 16)
                else:
                    act.dma_start(out[bass.ds(no(i, c) * BLOCK, 2 * BLOCK), :].rearrange("(b p j) f -> p b (j f)", b=2, j=TILES),
                                  o_t[:, 2 * k:2 * k + 2, :, :].rearrange("p b j f -> p b (j f)")).then_inc(stored[k], 16)

            def deviations(i, c):
                k = c // BATCH
                act.wait_ge(stats_ready, i * (U // BATCH) + k + 1)
                sc.activation(std[:, k, :], stats[:, k, :, 2], ACT.Sqrt, bias=lneps[:],
                              scale=1.0 / D).then_inc(std_ready, 1)

            def normalise(i, c):
                k = c // BATCH
                o = (c % BATCH) * (TILES + WINS)
                s = c % H_SLOTS
                act.wait_ge(scales_ready, i * (U // BATCH) + k + 1)
                at_least(act, psh_ready, no(i, c) - H_SLOTS + 1)
                for j in range(TILES):
                    last = sc.activation(h_t[:, c % H_SLOTS, j, :], x_t[:, c, j, :], ACT.Relu,
                                         bias=nbias[:, k, o + j:o + j + 1], scale=rstd[:, k, o + j:o + j + 1])
                last.then_inc(h_ready, 1)

            def edge_high(i, c):
                s = c % 4
                act.wait_ge(v_ready, no(i, c) + 1)
                at_least(act, psh_ready, no(i, c) - 3)
                sc.activation(m_hi[:, s, :, :], z_t[:, c % H_SLOTS, :, :], ACT.Relu).then_inc(hi_ready, 1)

            def copy_h(i, c):
                act.wait_ge(psh_ready, no(i, c) + 1)
                at_least(act, psu_ready, no(i, c) - 3)
                sc.activation(hT[:, c % 4, :], ps_h[c % 2][:], ACT.Copy).then_inc(hT_ready, 1)

            def bias_relu(i, c):
                act.wait_ge(psu_ready, no(i, c) + 1)
                at_least(act, pso_ready, no(i, c) - 3)
                sc.activation(uT[:, c % 4, :], ps_u[c % 2][:], ACT.Relu, bias=b1_sb[:]).then_inc(uT_ready, 1)

            act.wait_ge(s_prm, 80)
            act.wait_ge(s_pool, 3)

            def step(i, c):
                if (c - STORE_LAG) % 2 == 0:
                    run(store, i, c, STORE_LAG)
                run(copy_h, i, c, COPY_LAG)
                if c % BATCH == BATCH - 1:
                    run(deviations, i, c)
                run(normalise, i, c, NORM_LAG)
                run(bias_relu, i, c, RELU_LAG)
                run(edge_high, i, c, HIGH_LAG)

            def in_any_order():
                with act.Fori(0, G_ROUNDS) as t:
                    act.wait_ge(g_var, t + 1)
                    sc.activation(g_sd[0:GE, 0:1], g_mv[0:GE, 0, 1:2], ACT.Sqrt, bias=lneps[0:GE, :]).then_inc(g_std, 1)

                def dense(n):
                    act.wait_ge(g_var, G_ROUNDS + n + 1)
                    sc.activation(g_sd[:], g_mv[:, :, 1], ACT.Sqrt, bias=lneps[:]).then_inc(g_std, 1)
                    act.wait_ge(g_psh, n + 1)
                    sc.activation(hT[:, 0, :], ps_h[0][:], ACT.Copy).then_inc(g_hT, 1)
                    act.wait_ge(g_psu, n + 1)
                    sc.activation(uT[:, 0, :], ps_u[0][:], ACT.Relu, bias=b1_sb[:]).then_inc(g_uT, 1)

                with act.Fori(0, LAST) as n:
                    dense(n)
                dense(LAST)

            with act.If(ordinary(act) == 0):
                pipeline(act, step, STORE_LAG)
                act.wait_ge(stored[0], 16 * (N_BLOCKS // 4))
                act.wait_ge(stored[1], 16 * (N_BLOCKS // 4 + 1))
            with act.Else():
                in_any_order()

        @block.tensor
        def _(pe):
            te = nc.tensor
            pe.wait_ge(s_cut, 1)
            for q in range(4):
                te.matmul(cut_psum(q)[:, 0:EC], cut[:, 128 * q:128 * q + 128], dst_f[:], start=True, stop=True)
                last = te.matmul(cut_psum(q)[:, EC:EC + 1], below[:, 128 * q:128 * q + 128], e_c[:],
                                 start=True, stop=True)
            last.then_inc(s_rows, 1)
            pe.wait_ge(s_pos, 1)
            pe.wait_ge(s_cut, 2)
            pe.wait_ge(s_pool, 3)
            for q in range(4):
                te.matmul(ps_a[0:1, 128 * q:128 * q + 128], pos[:, q:q + 1], ident[:], start=True, stop=True)
            te.matmul(ps_b[0:1, 0:1], viols[:], ones[0:EP, 0:1], start=True, stop=True).then_inc(s_posT, 1)

            def transpose_and_sum(i, c):
                s = c % 4
                ps = ps_h[c % 2]
                pe.wait_ge(h_ready, no(i, c) + 1)
                at_least(pe, hT_ready, no(i, c) - 1)
                for j in range(TILES):
                    te.matmul(ps[:, 128 * j:128 * j + 128], h_t[:, c % H_SLOTS, j, :], ident[:], is_transpose=True,
                              start=(j == 0), stop=False, skip_group_check=True)
                pe.wait_ge(sel_ready, no(i, c) + 1)
                pe.wait_ge(lo_ready, no(i, c) + 1)
                for w in range(WINS):
                    o = ps[:, :].rearrange("p (j q) -> p j q", j=TILES)[:, :, WP * w:WP * w + WP]
                    for part in (m_hi, m_lo):
                        last = te.matmul(o, part[:, s, w, :], sel[:, s, w, :, :], start=False,
                                         stop=(w == WINS - 1 and part is m_lo), skip_group_check=True)
                last.then_inc(psh_ready, 1)

            def up(i, c):
                pe.wait_ge(hT_ready, no(i, c) + 1)
                at_least(pe, uT_ready, no(i, c) - 1)
                te.matmul(ps_u[c % 2][:], w1s[:], hT[:, c % 4, :], start=True, stop=True).then_inc(psu_ready, 1)

            def down(i, c):
                ps = ps_o[c % 2]
                at_least(pe, o_ready, no(i, c) - 1)
                te.matmul(ps[:], b2_ones[:], b2_rows[:, :, :].rearrange("p j f -> p (j f)"), start=True, stop=False,
                          skip_group_check=True)
                pe.wait_ge(uT_ready, no(i, c) + 1)
                for j in range(TILES):
                    last = te.matmul(ps[:, 128 * j:128 * j + 128], uT[:, c % 4, 128 * j:128 * j + 128], w2_sb[:],
                                     start=False, stop=(j == TILES - 1), skip_group_check=True)
                last.then_inc(pso_ready, 1)

            pe.wait_ge(s_prm, 80)
            pe.wait_ge(s_der, 1)

            def step(i, c):
                run(transpose_and_sum, i, c, PE_LAG)
                run(up, i, c, UP_LAG)
                run(down, i, c, DOWN_LAG)

            def in_any_order():
                with pe.Fori(0, G_ROUNDS) as t:
                    pe.wait_ge(g_msg, t + 1)
                    te.matmul(ps_a[0:GE, 0:D], g_same, z_t[0:GE, 0, 0, :], start=True, stop=True).then_inc(g_psum, 1)

                def dense(n):
                    pe.wait_ge(g_h, n + 1)
                    for j in range(TILES):
                        last = te.transpose(ps_h[0][:, 128 * j:128 * j + 128], h_t[:, 0, j, :], ident[:])
                    last.then_inc(g_psh, 1)
                    pe.wait_ge(g_hT, n + 1)
                    te.matmul(ps_u[0][:], w1_sb[:], hT[:, 0, :], start=True, stop=True).then_inc(g_psu, 1)
                    pe.wait_ge(g_uT, n + 1)
                    te.matmul(ps_o[0][:], b2_ones[:], b2_rows[:, :, :].rearrange("p j f -> p (j f)"),
                              start=True, stop=False, skip_group_check=True)
                    for j in range(TILES):
                        last = te.matmul(ps_o[0][:, 128 * j:128 * j + 128], uT[:, 0, 128 * j:128 * j + 128], w2_sb[:],
                                         start=False, stop=(j == TILES - 1), skip_group_check=True)
                    last.then_inc(g_pso, 1)

                with pe.Fori(0, LAST) as n:
                    dense(n)
                dense(LAST)

            with pe.If(ordinary(pe) == 0):
                pipeline(pe, step, DOWN_LAG)
            with pe.Else():
                in_any_order()


def kernel(x, src, dst, edge_attr_128, L0_gnn_W1, L0_gnn_b1, L0_gnn_W2, L0_gnn_b2, L0_gnn_eps):
    import numpy as np
    import concourse.bacc as bacc
    from concourse.bass_utils import run_bass_kernel_spmd

    nc = bacc.Bacc("TRN2", target_bir_lowering=False, num_devices=1)
    arrays = {
        "x": np.ascontiguousarray(x),
        "pairs": np.ascontiguousarray(np.stack([np.asarray(src), np.asarray(dst)], axis=1)),
        "dst": np.ascontiguousarray(dst),
        "edge_attr": np.ascontiguousarray(edge_attr_128),
        "w1": np.ascontiguousarray(L0_gnn_W1),
        "b1": np.ascontiguousarray(L0_gnn_b1),
        "w2": np.ascontiguousarray(L0_gnn_W2),
        "b2": np.ascontiguousarray(L0_gnn_b2),
        "eps": np.asarray(L0_gnn_eps).reshape(1),
    }
    args = [nc.dram_tensor("in_" + k, a.shape, mybir.dt.from_np(a.dtype), kind="ExternalInput").ap()
            for k, a in arrays.items()]
    out = nc.dram_tensor("out", (NODES, D), mybir.dt.float32, kind="ExternalOutput").ap()
    gnn_layer(nc, *args, out)
    got = run_bass_kernel_spmd(nc, [{"in_" + k: a for k, a in arrays.items()}], core_ids=[0])
    return got.results[0]["out"]
```

```python
import concourse.bass as bass
from concourse import mybir
from contextlib import ExitStack

NODES = 100000
EDGES = 25000
D = 128
LN_EPS = 1e-5

TILES = 4
BLOCK = 128 * TILES
N_BLOCKS = -(-NODES // BLOCK)
LAST = N_BLOCKS - 1
LAST_BASE = NODES - BLOCK
LAST_P0 = (LAST * BLOCK - LAST_BASE) // TILES
WINS = 2
WNODES = BLOCK // WINS
WP = 128 // WINS
WIN_EDGES = 128
STARTS = N_BLOCKS * WINS
SC = STARTS // 4
MID = 195
assert (NODES - 1) // WNODES - MID < 256 and STARTS - MID <= 256
EP, EC = 125, 200
EARLY = 8
U = 20
H_SLOTS = 10
GE = 125
G_ROUNDS = EDGES // GE
ZERO = 10240
ZERO_DMAS = NODES // 125 * D // ZERO
G_STEPS = 10
G_DENSE = 4
BATCH = 4
NORM_LAG = 5
SUM_LAG = 6
HIGH_LAG = 7
LOW_LAG = 8
PE_LAG = 9
COPY_LAG = 10
UP_LAG = 11
RELU_LAG = 12
DOWN_LAG = 13
ADD_LAG = 14
STORE_LAG = 16
EDGE_LAG = 8


def gnn_layer(nc, x, pairs, dst_flat, edge_attr, w1, b1, w2, b2, eps, out):
    fp32 = mybir.dt.float32
    fp32r = mybir.dt.float32r
    bf16 = mybir.dt.bfloat16
    i32 = mybir.dt.int32
    ALU = mybir.AluOpType
    ACT = mybir.ActivationFunctionType
    AX = mybir.AxisListType

    agg = nc.dram_tensor("agg", (NODES, D), fp32).ap()

    ctx = ExitStack()
    with ctx:
        def sb(name, shape, dt):
            return ctx.enter_context(nc.sbuf_tensor(name, shape, dt))

        def pb(name, shape, dt):
            return ctx.enter_context(nc.psum_tensor(name, shape, dt))

        def sem(name):
            return ctx.enter_context(nc.semaphore(name))

        x_t = sb("x_t", [128, U, TILES, D], fp32)
        pair_t = sb("pair_t", [128, U, WINS, 2], i32)
        ea_t = sb("ea_t", [128, U, WINS, D], fp32)
        xs_t = sb("xs_t", [128, U, WINS, D], fp32)
        h_t = sb("h_t", [128, H_SLOTS, TILES, D], fp32)
        z_t = sb("z_t", [128, H_SLOTS, WINS, D], fp32)
        m_hi = sb("m_hi", [128, 4, WINS, D], fp32r)
        m_lo = sb("m_lo", [128, 4, WINS, D], fp32r)
        sel = sb("sel", [128, 4, WINS, TILES, WP], fp32r)
        rel = sb("rel", [128, U, WINS], fp32)
        hT = sb("hT", [128, 4, BLOCK], fp32)
        uT = sb("uT", [128, 4, BLOCK], fp32)
        o_t = sb("o_t", [128, 4, TILES, D], fp32)
        NS = BATCH * (TILES + WINS)
        stats = sb("stats", [128, U // BATCH, NS, 3], fp32)
        std = sb("std", [128, U // BATCH, NS], fp32)
        rstd = sb("rstd", [128, U // BATCH, NS], fp32)
        nbias = sb("nbias", [128, U // BATCH, NS], fp32)
        ident = sb("ident", [128, 128], fp32)
        ones = sb("ones", [128, 128], fp32)
        w1_sb = sb("w1_sb", [D, D], fp32)
        w2_sb = sb("w2_sb", [D, D], fp32)
        b1_sb = sb("b1_sb", [D, 1], fp32)
        b2_sb = sb("b2_sb", [128, 3, D], fp32)
        b2_part = sb("b2_part", [128, 2, D], bf16)
        b2_rows = sb("b2_rows", [128, TILES, D], bf16)
        b2_ones = sb("b2_ones", [128, 128], bf16)
        eps_sb = sb("eps_sb", [128, 1], fp32)
        opeps = sb("opeps", [128, 1], fp32)
        lneps = sb("lneps", [128, 1], fp32)
        offs = sb("offs", [128, TILES, WP], fp32)
        base = sb("base", [128, U, WINS], fp32)
        dst_i = sb("dst_i", [EP, EC + 1], i32)
        dst_w = sb("dst_w", [EP, EC + 1], i32)
        dst_b = sb("dst_b", [EP, EC + 2], bf16)
        ends = sb("ends", [EP, 2], fp32)
        ends_off = sb("ends_off", [EP, 2], fp32)
        t_row = sb("t_row", [EP, STARTS], bf16)
        t_col = sb("t_col", [SC, 4], fp32)
        below = sb("below", [EP, STARTS], bf16)
        cut = sb("cut", [EP, STARTS], bf16)
        less = sb("less", [SC, 4, EC], fp32)
        cnt = sb("cnt", [SC, 4], fp32)
        pos = sb("pos", [SC, 4], fp32)
        viol = sb("viol", [EP, EC], fp32)
        viols = sb("viols", [EP, 1], fp32)
        row = sb("row", [1, STARTS], fp32)
        gap = sb("gap", [1, STARTS], fp32)
        low = sb("low", [1, 3], fp32)
        starts = sb("starts", [1, STARTS], i32)
        flag = sb("flag", [1, 1], i32)

        ps_h = [pb(f"ps_h{i}", [128, BLOCK], fp32) for i in range(2)]
        ps_u = [pb(f"ps_u{i}", [128, BLOCK], fp32) for i in range(2)]
        ps_o = [pb(f"ps_o{i}", [128, BLOCK], fp32) for i in range(2)]
        ps_a = pb("ps_a", [128, 512], fp32)
        ps_b = pb("ps_b", [128, 512], fp32)

        s_dst = sem("dst_loaded")
        s_prm = sem("params_loaded")
        s_pool = sem("pool_constants")
        s_dve = sem("dve_chain")
        pairs_seen = sem("pairs_seen")
        scales_seen = sem("scales_seen")
        s_b2 = sem("b2_split")
        x_seen = sem("x_seen")
        s_der = sem("b2_rows_ready")
        s_cut = sem("cuts_ready")
        s_viol = sem("order_checked")
        s_early = sem("early_stats_done")
        s_rows = sem("cut_rows_ready")
        s_pos = sem("positions_ready")
        s_posT = sem("positions_row_ready")
        s_flag = sem("starts_and_flag_ready")
        x_loaded = [sem(f"x_loaded{i}") for i in range(U // 2)]
        pair_loaded = [sem(f"pair_loaded{i}") for i in range(U)]
        ea_loaded = [sem(f"ea_loaded{i}") for i in range(U)]
        xs_gathered = [sem(f"xs_gathered{i}") for i in range(U)]
        stored = [sem(f"stored{i}") for i in range(2)]
        stats_ready = sem("stats_ready")
        std_ready = sem("std_ready")
        rstd_ready = sem("rstd_ready")
        scales_ready = sem("scales_ready")
        h_ready = sem("h_ready")
        z_ready = sem("z_ready")
        v_ready = sem("v_ready")
        hi_ready = sem("hi_ready")
        lo_ready = sem("lo_ready")
        rel_ready = sem("rel_ready")
        base_ready = sem("base_ready")
        sel_ready = sem("sel_ready")
        psh_ready = sem("psh_ready")
        hT_ready = sem("hT_ready")
        psu_ready = sem("psu_ready")
        uT_ready = sem("uT_ready")
        pso_ready = sem("pso_ready")
        o_ready = sem("o_ready")

        g_stats = sb("g_stats", [128, TILES, 6], fp32)
        g_mv = sb("g_mv", [128, TILES, 2], fp32)
        g_sd = sb("g_sd", [128, TILES], fp32)
        g_rstd = sb("g_rstd", [128, TILES], fp32)
        g_any_t = sb("g_any_t", [128, 2], fp32)
        g_idx_t = sb("g_idx_t", [128, 1], i32)
        t_idx = sb("t_idx", [128, 1], fp32)
        g_col_t = sb("g_col_t", [128, 128], fp32)
        g_idx, g_any, g_dst = g_idx_t[0:GE, :], g_any_t[0:GE, 0:1], g_any_t[0:GE, 1:2]
        g_col = g_col_t[0:GE, 0:GE]
        g_rows = sb("g_rows", [128, 5, 128], fp32)
        g_row, g_same, g_dup, g_before = (g_rows[0:GE, k, 0:GE] for k in range(4))
        g_row_i = g_rows[0:GE, 4, 0:GE].bitcast(i32)
        agg_flat = agg.rearrange("(p n) f -> p (n f)", p=125)
        zeros = x_t[0:125, :, :, :].rearrange("p u j f -> p (u j f)")[:, 0:ZERO]
        g_zeroed = sem("g_zeroed")
        g_zeros, g_agg, g_in, g_xs, g_dve = (sem("g_" + k) for k in ("zeros", "agg", "in", "xs", "dve"))
        g_var, g_std, g_msg, g_psum, g_sum = (sem("g_" + k) for k in ("var", "std", "msg", "psum", "sum"))
        g_x, g_h, g_psh, g_hT, g_psu, g_uT = (sem("g_" + k) for k in ("x", "h", "psh", "hT", "psu", "uT"))
        g_pso, g_o, g_stored, g_free = (sem("g_" + k) for k in ("pso", "o", "stored", "free"))

        block = ctx.enter_context(nc.Block())

        def cut_psum(q, n=1):
            return ps_h[q // 2][0:SC, q % 2 * (EC + 1):(q % 2 + n) * (EC + 1)]

        def ordinary(eng):
            eng.wait_ge(s_flag, 1)
            return eng.value_load(flag[0:1, 0:1], min_val=0, max_val=3)

        def pipeline(eng, step, lag):
            for c in range(U):
                step(0, c)
            with eng.Fori(1, N_BLOCKS // U) as i:
                for c in range(U):
                    step(i, c)
            for n in range(N_BLOCKS // U * U, N_BLOCKS + lag):
                step(n // U, n % U)

        def run(stage, i, c, lag=0):
            i, c = i + (c - lag) // U, (c - lag) % U
            if not isinstance(i, int) or 0 <= i * U + c < N_BLOCKS:
                stage(i, c)

        def is_last(i, c):
            return isinstance(i, int) and i * U + c == LAST

        def is_early(i, c):
            return isinstance(i, int) and i * U + c < EARLY

        def no(i, c):
            return i * U + c

        def at_least(eng, sem, value):
            if not isinstance(value, int) or value > 0:
                eng.wait_ge(sem, value)

        def load_x(eng, i, c):
            if isinstance(i, int) and no(i, c) == LAST - 1:
                for b, first in ((0, no(i, c) * BLOCK), (1, LAST_BASE)):
                    eng.dma_start(x_t[:, c + b, :, :], x[first:first + BLOCK, :].rearrange("(p j) f -> p j f", j=TILES)
                                  ).then_inc(x_loaded[c // 2], 16)
            else:
                eng.dma_start(x_t[:, c:c + 2, :, :].rearrange("p b j f -> p b (j f)"),
                              x[bass.ds(no(i, c) * BLOCK, 2 * BLOCK), :].rearrange("(b p j) f -> p b (j f)", b=2, j=TILES)
                              ).then_inc(x_loaded[c // 2], 16)

        @block.sync
        def _(sp):
            dst_rows = dst_flat.rearrange("(p c) -> p c", c=EC)
            nc.sync.dma_start(dst_i[:, 1:EC + 1], dst_rows).then_inc(s_dst, 16)
            sp.wait_ge(s_pool, 1)
            with nc.allow_non_contiguous_dma(reason="124 elements once"):
                nc.sync.dma_start(dst_i[1:EP, 0:1], dst_rows[0:EP - 1, EC - 1:EC]).then_inc(s_dst, 16)

            for c in range(0, U, 2):
                load_x(sp, 0, c)

            start_regs = [sp.alloc_register(f"window_start{w}") for w in range(2 * WINS)]

            def load_windows(i, c):
                at_least(sp, v_ready, no(i, c) - U + 2)
                sp.load(start_regs, starts[0:1, bass.ds(no(i, c) * WINS, 2 * WINS)])
                for b in range(2):
                    for w in range(WINS):
                        s = sp.snap(start_regs[b * WINS + w], min_val=0, max_val=EDGES - WIN_EDGES)
                        sp.dma_start(pair_t[:, c + b, w, :], pairs[bass.ds(s, WIN_EDGES), :]).then_inc(pair_loaded[c + b], 16)
                        sp.dma_start(ea_t[:, c + b, w, :], edge_attr[bass.ds(s, WIN_EDGES), :]).then_inc(ea_loaded[c + b], 16)

            def step(i, c):
                if c % 2 == 0:
                    run(load_windows, i, c)

            def in_any_order():
                sp.wait_ge(g_zeros, 1)
                for k in range(ZERO_DMAS):
                    sp.dma_start(agg_flat[:, k * ZERO:k * ZERO + ZERO], zeros).then_inc(g_zeroed, 16)
                sp.wait_ge(g_zeroed, 16 * ZERO_DMAS)

                def load_round(t):
                    rows = bass.ds(t * GE, GE)
                    sp.dma_start(pair_t[0:GE, 0, 0, :], pairs[rows, :]).then_inc(g_in, 16)
                    sp.dma_start(ea_t[0:GE, 0, 0, :], edge_attr[rows, :]).then_inc(g_in, 16)
                    sp.dma_start(g_row_i, dst_flat[rows].rearrange("(o e) -> o e", o=1).to_broadcast([GE, GE])
                                 ).then_inc(g_in, 16)

                load_round(0)
                with sp.Fori(1, G_ROUNDS) as t:
                    sp.wait_ge(g_agg, 16 * t)
                    sp.sem_inc(g_free, 1)
                    load_round(t)
                sp.wait_ge(g_agg, 16 * G_ROUNDS)

                def dense(n):
                    first = LAST_BASE if n is LAST else n * BLOCK
                    p0 = LAST_P0 if n is LAST else 0
                    rows = bass.ds(first, BLOCK)
                    sp.dma_start(x_t[:, 0, :, :], x[rows, :].rearrange("(p j) f -> p j f", j=TILES)).then_inc(g_x, 16)
                    sp.dma_start(x_t[:, 1, :, :], agg[rows, :].rearrange("(p j) f -> p j f", j=TILES)).then_inc(g_x, 16)
                    sp.wait_ge(g_o, n + 1)
                    sp.dma_start(out[bass.ds(n * BLOCK, BLOCK - TILES * p0), :].rearrange("(p j) f -> p (j f)", j=TILES),
                                 o_t[p0:128, 0, :, :].rearrange("p j f -> p (j f)")).then_inc(g_stored, 16)
                    sp.wait_ge(g_stored, 16 * n + 16)
                    sp.sem_inc(g_free, 1)

                with sp.Fori(0, LAST) as n:
                    dense(n)
                dense(LAST)

            with sp.If(ordinary(sp) == 0):
                pipeline(sp, step, 0)
            with sp.Else():
                in_any_order()

        @block.gpsimd
        def _(pool):
            def iota(tile, pattern, first=0, by_partition=0):
                return nc.gpsimd.iota(tile, pattern, base=first, channel_multiplier=by_partition,
                                      allow_small_or_imprecise_dtypes=True)

            nc.gpsimd.memset(dst_i[:, 0:1], -1).then_inc(s_pool, 1)
            iota(t_idx[:], [[0, 1]], by_partition=1)
            nc.gpsimd.memset(ends_off[:], -float(MID)).then_inc(s_pool, 1)
            iota(dst_b[:, EC + 1:EC + 2], [[0, 1]], by_partition=1)
            iota(t_row[:], [[1, STARTS]], first=-MID)
            iota(t_col[:], [[SC, 4]], first=-MID, by_partition=1).then_inc(s_pool, 1)
            nc.gpsimd.memset(lneps[:], LN_EPS)
            nc.gpsimd.memset(ones[:], 1.0).then_inc(s_pool, 1)
            pool.wait_ge(s_pool, 4)
            nc.gpsimd.affine_select(out=ident[:], in_=ones[:], compare_op=ALU.is_equal, fill=0.0, base=0,
                                    pattern=[[-1, 128]], channel_multiplier=1).then_inc(s_pool, 1)
            nc.gpsimd.memset(b2_rows[:], 0.0)
            nc.gpsimd.memset(b2_ones[:], 1.0).then_inc(s_pool, 1)
            iota(base[:], [[WNODES, U * WINS]])
            iota(offs[:], [[1, TILES], [TILES, WP]])
            iota(g_col_t[:], [[1, 128]]).then_inc(s_pool, 1)

            def gather(i, c):
                pool.wait_ge(pair_loaded[c], 16 * WINS * (i + 1))
                pool.sem_inc(pairs_seen, 1)
                for w in range(WINS):
                    pool.indirect_dma_start(
                        out=xs_t[:, c, w, :], out_offset=None, in_=x,
                        in_offset=bass.IndirectOffsetOnAxis(ap=pair_t[:, c, w, 0:1], axis=0),
                    ).then_inc(xs_gathered[c], 16)

            def normalise_edges(i, c):
                k = c // BATCH
                at_least(pool, lo_ready, no(i, c) - H_SLOTS + 1)
                pool.wait_ge(scales_ready, i * (U // BATCH) + k + 1)
                pool.sem_inc(scales_seen, 1)
                for w in range(WINS):
                    q = c % BATCH * (TILES + WINS) + TILES + w
                    last = nc.gpsimd.tensor_scalar(z_t[:, c % H_SLOTS, w, :], xs_t[:, c, w, :], rstd[:, k, q:q + 1],
                                                   nbias[:, k, q:q + 1], ALU.mult, ALU.add)
                last.then_inc(z_ready, 1)

            def step(i, c):
                run(gather, i, c)
                run(normalise_edges, i, c, EDGE_LAG)

            def in_any_order():
                with pool.Fori(0, G_ROUNDS) as t:
                    pool.wait_ge(g_in, 48 * t + 48)
                    pool.sem_inc(pairs_seen, 1)
                    pool.indirect_dma_start(
                        out=xs_t[0:GE, 0, 0, :], out_offset=None, in_=x,
                        in_offset=bass.IndirectOffsetOnAxis(ap=pair_t[0:GE, 0, 0, 0:1], axis=0)).then_inc(g_xs, 16)
                    pool.indirect_dma_start(
                        out=xs_t[0:GE, 0, 1, :], out_offset=None, in_=agg,
                        in_offset=bass.IndirectOffsetOnAxis(ap=pair_t[0:GE, 0, 0, 1:2], axis=0)).then_inc(g_xs, 16)
                    pool.wait_ge(g_sum, t + 1)
                    pool.sem_inc(scales_seen, 1)
                    pool.indirect_dma_start(
                        out=agg, out_offset=bass.IndirectOffsetOnAxis(ap=g_idx, axis=0), in_=xs_t[0:GE, 0, 1, :],
                        in_offset=None, bounds_check=NODES - 1, oob_is_err=False).then_inc(g_agg, 16)

            with pool.If(ordinary(pool) == 0):
                pipeline(pool, step, EDGE_LAG)
            with pool.Else():
                in_any_order()

        @block.vector
        def _(dve):
            ve = nc.vector
            chain = [0]

            def link(ins):
                chain[0] += 1
                ins.then_inc(s_dve, 1)
                dve.wait_ge(s_dve, chain[0])

            def node_stats(i, c):
                k = c // BATCH
                o = (c % BATCH) * (TILES + WINS)
                dve.wait_ge(x_loaded[c // 2], 16 * (i + (2 if isinstance(i, int) and no(i, c) >= LAST - 1 else 1)))
                for j in range(0, TILES, 2):
                    last = ve.bn_stats(stats[:, k, o + j:o + j + 2, :].rearrange("p a b -> p (a b)"),
                                       x_t[:, c, j:j + 2, :].rearrange("p j f -> p f j"))
                return last

            dve.wait_ge(s_pool, 2)
            link(ve.tensor_scalar(viols[:], t_idx[0:EP, :], EP - 1.5, float(2 * STARTS), ALU.is_gt, ALU.mult))
            link(ve.tensor_tensor(ends_off[:, 1:2], ends_off[:, 1:2], viols[:], ALU.add))
            dve.wait_ge(s_dst, 32)
            link(ve.tensor_scalar(dst_w[:], dst_i[:], WNODES.bit_length() - 1, None, ALU.arith_shift_right))
            ve.tensor_tensor(ends[:], dst_w[:, 0:EC + 1:EC], ends_off[:], ALU.add)
            dve.wait_ge(s_pool, 3)
            link(ve.tensor_scalar(dst_b[:, 0:EC + 1], dst_w[:], -float(MID), None, ALU.add))
            ve.tensor_scalar(below[:], t_row[:], ends[:, 1:2], None, ALU.is_gt)
            link(ve.tensor_scalar(cut[:], t_row[:], ends[:, 0:1], None, ALU.is_gt))
            ve.tensor_tensor(cut[:], cut[:], below[:], ALU.subtract).then_inc(s_cut, 1)
            link(ve.tensor_tensor(viol[:], dst_i[:, 1:EC + 1], dst_i[:, 0:EC], ALU.is_lt))
            ve.tensor_reduce(viols[:], viol[:], AX.X, ALU.add).then_inc(s_viol, 1)
            dve.wait_ge(s_prm, 80)
            link(ve.tensor_scalar(opeps[:], eps_sb[:], 1.0, None, ALU.add))
            ve.tensor_scalar(low[:, 2:3], opeps[0:1, :], 0.0, None, ALU.is_lt)
            for q in (0, 2):
                dve.wait_ge(s_rows, q // 2 + 1)
                last = ve.tensor_tensor(less[:, q:q + 2, :], cut_psum(q, 2).rearrange("p (q e) -> p q e", q=2)[:, :, 0:EC],
                                        t_col[:, q:q + 2].unsqueeze(2).broadcast_to([SC, 2, EC]), ALU.is_lt)
            link(last)
            link(ve.tensor_reduce(cnt[:], less[:], AX.X, ALU.add))
            for q in (0, 2):
                last = ve.scalar_tensor_tensor(out=pos[:, q:q + 2], scalar=float(EC), in1=cnt[:, q:q + 2],
                                               in0=cut_psum(q, 2).rearrange("p (q e) -> p q e", q=2)[:, :, EC],
                                               op0=ALU.mult, op1=ALU.add)
            last.then_inc(s_pos, 1)
            link(ve.tensor_copy(b2_part[:, 0, :], b2_sb[:, 0, :]))
            link(ve.tensor_tensor(b2_sb[:, 1, :], b2_sb[:, 0, :], b2_part[:, 0, :], ALU.subtract))
            link(ve.tensor_copy(b2_part[:, 1, :], b2_sb[:, 1, :]))
            ve.tensor_tensor(b2_sb[:, 2, :], b2_sb[:, 1, :], b2_part[:, 1, :], ALU.subtract).then_inc(s_b2, 1)
            dve.wait_ge(s_posT, 1)
            link(ve.tensor_copy(row[:], ps_a[0:1, 0:STARTS]))
            ve.tensor_tensor(gap[:, 0:STARTS - 1], row[:, 1:STARTS], row[:, 0:STARTS - 1], ALU.subtract)
            link(ve.scalar_tensor_tensor(out=low[:, 1:2], in0=ps_b[0:1, 0:1], scalar=0.5, in1=low[:, 2:3],
                                         op0=ALU.is_gt, op1=ALU.add))
            link(ve.tensor_reduce(low[:, 0:1], gap[:, 0:STARTS - 1], AX.X, ALU.max))
            ve.tensor_scalar(starts[:], row[:], float(EDGES - WIN_EDGES), None, ALU.min)
            ve.scalar_tensor_tensor(out=flag[:], in0=low[:, 0:1], scalar=WIN_EDGES + 0.5, in1=low[:, 1:2],
                                    op0=ALU.is_gt, op1=ALU.add).then_inc(s_flag, 1)
            for c in range(EARLY):
                last = node_stats(0, c)
            last.then_inc(s_early, 1)

            def rows_stats(i, c):
                k = c // BATCH
                o = (c % BATCH) * (TILES + WINS)
                if not is_early(i, c):
                    node_stats(i, c)
                dve.wait_ge(xs_gathered[c], 16 * WINS * (i + 1))
                last = ve.bn_stats(stats[:, k, o + TILES:o + TILES + WINS, :].rearrange("p a b -> p (a b)"),
                                   xs_t[:, c, :, :].rearrange("p j f -> p f j"))
                if c % BATCH == BATCH - 1:
                    last.then_inc(stats_ready, 1)

            def scales(i, c):
                k = c // BATCH
                q = i * (U // BATCH) + k + 1
                dve.wait_ge(std_ready, q)
                ve.reciprocal(rstd[:, k, :], std[:, k, :]).then_inc(rstd_ready, 1)
                dve.wait_ge(rstd_ready, 2 * q - 1)
                rn = rstd[:, k, :].rearrange("p (b r) -> p b r", b=BATCH)[:, :, 0:TILES]
                ve.tensor_scalar(rn, rn, opeps[:], None, ALU.mult).then_inc(rstd_ready, 1)
                dve.wait_ge(rstd_ready, 2 * q)
                ve.scalar_tensor_tensor(out=nbias[:, k, :], in0=stats[:, k, :, 1], scalar=-1.0, in1=rstd[:, k, :],
                                        op0=ALU.mult, op1=ALU.mult).then_inc(scales_ready, 1)

            def edge_sum(i, c):
                dve.wait_ge(z_ready, no(i, c) + 1)
                dve.wait_ge(ea_loaded[c], 16 * WINS * (i + 1))
                ve.scalar_tensor_tensor(out=z_t[:, c % H_SLOTS, :, :], in0=z_t[:, c % H_SLOTS, :, :], scalar=0.0, in1=ea_t[:, c, :, :],
                                        op0=ALU.max, op1=ALU.add).then_inc(v_ready, 1)

            def edge_low(i, c):
                s = c % 4
                dve.wait_ge(hi_ready, no(i, c) + 1)
                ve.scalar_tensor_tensor(out=m_lo[:, s, :, :], in0=z_t[:, c % H_SLOTS, :, :], scalar=0.0,
                                        in1=m_hi[:, s, :, :].bitcast(fp32),
                                        op0=ALU.max, op1=ALU.subtract).then_inc(lo_ready, 1)

            def relative(i, c):
                if c == BATCH - 1 and not (isinstance(i, int) and i == 0):
                    dve.wait_ge(rel_ready, i * (U // BATCH))
                    ve.tensor_scalar(base[:], base[:], float(U * BLOCK), None, ALU.add).then_inc(base_ready, 1)
                    dve.wait_ge(base_ready, i)
                first = c - BATCH + 1
                end = c if is_last(i, c) else c + 1
                last = ve.tensor_tensor(rel[:, first:end, :], pair_t[:, first:end, :, 1], base[:, first:end, :],
                                        ALU.subtract)
                if is_last(i, c):
                    for w in range(WINS):
                        last = ve.tensor_scalar(rel[:, c, w:w + 1], pair_t[:, c, w, 1:2],
                                                -float(LAST_BASE + w * WNODES), None, ALU.add)
                last.then_inc(rel_ready, 1)

            def select(i, c):
                s = c % 4
                dve.wait_ge(rel_ready, i * (U // BATCH) + c // BATCH + 1)
                at_least(dve, psh_ready, no(i, c) - 3)
                for w in range(WINS):
                    last = ve.tensor_scalar(sel[:, s, w, :, :], offs[:], rel[:, c, w:w + 1], None, ALU.is_equal)
                last.then_inc(sel_ready, 1)

            def add(i, c):
                s = c % 4
                dve.wait_ge(pso_ready, no(i, c) + 1)
                at_least(dve, stored[s // 2], 16 * (i * (U // 4) + c // 4))
                ve.tensor_tensor(o_t[:, s, :, :].rearrange("p j f -> p (j f)"), ps_o[c % 2][:],
                                 x_t[:, c, :, :].rearrange("p j f -> p (j f)"), ALU.add).then_inc(o_ready, 1)

            def step(i, c):
                run(rows_stats, i, c)
                run(add, i, c, ADD_LAG)
                if c % BATCH == 0:
                    run(scales, i, c, 1)
                run(select, i, c, LOW_LAG)
                run(edge_low, i, c, LOW_LAG)
                run(edge_sum, i, c, SUM_LAG)
                if (c - 1) % BATCH == BATCH - 1:
                    run(relative, i, c, 1)

            def in_any_order():
                dve.wait_ge(s_early, 1)
                for k in range(U // 2):
                    dve.wait_ge(x_loaded[k], 16)
                    dve.sem_inc(x_seen, 1)
                ve.memset(zeros, 0.0).then_inc(g_zeros, 1)
                ve.tensor_scalar(g_before, g_col, t_idx[0:GE, :], None, ALU.is_lt)

                with dve.Fori(0, G_ROUNDS) as t:
                    step_no = [0]

                    def then(ins):
                        step_no[0] += 1
                        ins.then_inc(g_dve, 1)
                        dve.wait_ge(g_dve, t * G_STEPS + step_no[0])

                    xs, ag, msg = xs_t[0:GE, 0, 0, :], xs_t[0:GE, 0, 1, :], z_t[0:GE, 0, 0, :]
                    st, mv = g_stats[0:GE, 0, :], g_mv[0:GE, 0, :]
                    dve.wait_ge(g_xs, 32 * t + 32)
                    then(ve.bn_stats(st, xs))
                    ve.tensor_copy(g_dst, pair_t[0:GE, 0, 0, 1:2])
                    ve.bn_aggr(mv, st).then_inc(g_var, 1)
                    dve.wait_ge(g_std, t + 1)
                    then(ve.reciprocal(g_rstd[0:GE, 0:1], g_sd[0:GE, 0:1]))
                    then(ve.tensor_scalar(msg, xs, mv[:, 0:1], g_rstd[0:GE, 0:1], ALU.subtract, ALU.mult))
                    then(ve.scalar_tensor_tensor(out=msg, in0=msg, scalar=0.0, in1=ea_t[0:GE, 0, 0, :],
                                                 op0=ALU.max, op1=ALU.add))
                    then(ve.tensor_scalar(msg, msg, 0.0, None, ALU.max))
                    then(ve.tensor_copy(g_row, g_row_i))
                    ve.tensor_scalar(g_same, g_row, g_dst, None, ALU.is_equal).then_inc(g_msg, 1)
                    dve.wait_ge(g_msg, t + 1)
                    then(ve.tensor_tensor(g_dup, g_same, g_before, ALU.mult))
                    then(ve.tensor_reduce(g_any, g_dup, AX.X, ALU.max))
                    then(ve.tensor_scalar(g_any, g_any, float(1 << 20), None, ALU.mult))
                    then(ve.tensor_tensor(g_idx, g_any, g_dst, ALU.add))
                    dve.wait_ge(g_psum, t + 1)
                    ve.tensor_tensor(ag, ps_a[0:GE, 0:D], ag, ALU.add).then_inc(g_sum, 1)
                    assert step_no[0] == G_STEPS

                def dense(n):
                    step_no = [0]

                    def then(ins):
                        step_no[0] += 1
                        ins.then_inc(g_dve, 1)
                        dve.wait_ge(g_dve, G_ROUNDS * G_STEPS + n * G_DENSE + step_no[0])

                    dve.wait_ge(g_x, 32 * n + 32)
                    for j in range(TILES):
                        last = ve.bn_stats(g_stats[:, j, :], x_t[:, 0, j, :])
                    then(last)
                    ve.tensor_copy(g_any_t[:, 0:1], t_idx[:])
                    for j in range(TILES):
                        last = ve.bn_aggr(g_mv[:, j, :], g_stats[:, j, :])
                    last.then_inc(g_var, 1)
                    dve.wait_ge(g_std, G_ROUNDS + n + 1)
                    then(ve.reciprocal(g_rstd[:], g_sd[:]))
                    for j in range(TILES):
                        last = ve.tensor_scalar(h_t[:, 0, j, :], x_t[:, 0, j, :], g_mv[:, j, 0:1], g_rstd[:, j:j + 1],
                                                ALU.subtract, ALU.mult)
                    then(last)
                    then(ve.tensor_scalar(h_t[:, 0, :, :], h_t[:, 0, :, :], 0.0, opeps[:], ALU.max, ALU.mult))
                    ve.tensor_tensor(h_t[:, 0, :, :], h_t[:, 0, :, :], x_t[:, 1, :, :], ALU.add).then_inc(g_h, 1)
                    dve.wait_ge(g_pso, n + 1)
                    ve.tensor_tensor(o_t[:, 0, :, :].rearrange("p j f -> p (j f)"), ps_o[0][:],
                                     x_t[:, 0, :, :].rearrange("p j f -> p (j f)"), ALU.add).then_inc(g_o, 1)
                    assert step_no[0] == G_DENSE

                with dve.Fori(0, LAST) as n:
                    dense(n)
                dense(LAST)

            dve.wait_ge(s_pool, 7)
            with dve.If(ordinary(dve) == 0):
                pipeline(dve, step, ADD_LAG)
            with dve.Else():
                in_any_order()

        @block.scalar
        def _(act):
            sc = nc.scalar

            def store(i, c):
                k = c % 4 // 2
                act.wait_ge(o_ready, no(i, c) + 2)
                if isinstance(i, int) and no(i, c) == LAST - 1:
                    act.dma_start(out[(LAST - 1) * BLOCK:LAST * BLOCK, :].rearrange("(p j) f -> p (j f)", j=TILES),
                                  o_t[:, 2 * k, :, :].rearrange("p j f -> p (j f)")).then_inc(stored[k], 16)
                    act.dma_start(out[LAST * BLOCK:NODES, :].rearrange("(p j) f -> p (j f)", j=TILES),
                                  o_t[LAST_P0:128, 2 * k + 1, :, :].rearrange("p j f -> p (j f)")).then_inc(stored[k], 16)
                else:
                    act.dma_start(out[bass.ds(no(i, c) * BLOCK, 2 * BLOCK), :].rearrange("(b p j) f -> p b (j f)", b=2, j=TILES),
                                  o_t[:, 2 * k:2 * k + 2, :, :].rearrange("p b j f -> p b (j f)")).then_inc(stored[k], 16)

            def deviations(i, c):
                k = c // BATCH
                act.wait_ge(stats_ready, i * (U // BATCH) + k + 1)
                sc.activation(std[:, k, :], stats[:, k, :, 2], ACT.Sqrt, bias=lneps[:],
                              scale=1.0 / D).then_inc(std_ready, 1)

            def normalise(i, c):
                k = c // BATCH
                o = (c % BATCH) * (TILES + WINS)
                s = c % H_SLOTS
                act.wait_ge(scales_ready, i * (U // BATCH) + k + 1)
                at_least(act, psh_ready, no(i, c) - H_SLOTS + 1)
                for j in range(TILES):
                    last = sc.activation(h_t[:, c % H_SLOTS, j, :], x_t[:, c, j, :], ACT.Relu,
                                         bias=nbias[:, k, o + j:o + j + 1], scale=rstd[:, k, o + j:o + j + 1])
                last.then_inc(h_ready, 1)

            def edge_high(i, c):
                s = c % 4
                act.wait_ge(v_ready, no(i, c) + 1)
                at_least(act, psh_ready, no(i, c) - 3)
                sc.activation(m_hi[:, s, :, :], z_t[:, c % H_SLOTS, :, :], ACT.Relu).then_inc(hi_ready, 1)

            def copy_h(i, c):
                act.wait_ge(psh_ready, no(i, c) + 1)
                at_least(act, psu_ready, no(i, c) - 3)
                sc.activation(hT[:, c % 4, :], ps_h[c % 2][:], ACT.Copy).then_inc(hT_ready, 1)

            def bias_relu(i, c):
                act.wait_ge(psu_ready, no(i, c) + 1)
                at_least(act, pso_ready, no(i, c) - 3)
                sc.activation(uT[:, c % 4, :], ps_u[c % 2][:], ACT.Relu, bias=b1_sb[:]).then_inc(uT_ready, 1)

            with nc.allow_non_contiguous_dma(reason="129 elements once"):
                act.dma_start(eps_sb[:], eps.rearrange("(o f) -> o f", o=1).to_broadcast([128, 1])).then_inc(s_prm, 16)
                act.dma_start(b1_sb[:], b1.rearrange("(p o) -> p o", o=1)).then_inc(s_prm, 16)
            act.dma_start(b2_sb[:, 0, :], b2.rearrange("(o f) -> o f", o=1).to_broadcast([128, D])).then_inc(s_prm, 16)
            act.dma_start(w1_sb[:], w1).then_inc(s_prm, 16)
            act.dma_start(w2_sb[:], w2).then_inc(s_prm, 16)
            act.wait_ge(s_prm, 80)
            act.wait_ge(s_pool, 6)
            act.wait_ge(s_b2, 1)
            for r, part in ((0, 0), (32, 1), (64, 2)):
                last = sc.activation(b2_rows[r:r + 1, :, :], b2_sb[r:r + 1, part, :].unsqueeze(1).broadcast_to([1, TILES, D]),
                                     ACT.Copy)
            last.then_inc(s_der, 1)

            def step(i, c):
                if (c - STORE_LAG) % 2 == 0:
                    run(store, i, c, STORE_LAG)
                    if not (isinstance(i, int) and i * U + c < STORE_LAG):
                        run(lambda i, c: load_x(act, i, c), i, c, STORE_LAG - U)
                run(copy_h, i, c, COPY_LAG)
                if c % BATCH == BATCH - 1:
                    run(deviations, i, c)
                run(normalise, i, c, NORM_LAG)
                run(bias_relu, i, c, RELU_LAG)
                run(edge_high, i, c, HIGH_LAG)

            def in_any_order():
                with act.Fori(0, G_ROUNDS) as t:
                    act.wait_ge(g_var, t + 1)
                    sc.activation(g_sd[0:GE, 0:1], g_mv[0:GE, 0, 1:2], ACT.Sqrt, bias=lneps[0:GE, :]).then_inc(g_std, 1)

                def dense(n):
                    act.wait_ge(g_var, G_ROUNDS + n + 1)
                    sc.activation(g_sd[:], g_mv[:, :, 1], ACT.Sqrt, bias=lneps[:]).then_inc(g_std, 1)
                    act.wait_ge(g_psh, n + 1)
                    sc.activation(hT[:, 0, :], ps_h[0][:], ACT.Copy).then_inc(g_hT, 1)
                    act.wait_ge(g_psu, n + 1)
                    sc.activation(uT[:, 0, :], ps_u[0][:], ACT.Relu, bias=b1_sb[:]).then_inc(g_uT, 1)

                with act.Fori(0, LAST) as n:
                    dense(n)
                dense(LAST)

            with act.If(ordinary(act) == 0):
                pipeline(act, step, STORE_LAG)
                act.wait_ge(stored[0], 16 * (N_BLOCKS // 4))
                act.wait_ge(stored[1], 16 * (N_BLOCKS // 4 + 1))
            with act.Else():
                in_any_order()

        @block.tensor
        def _(pe):
            te = nc.tensor
            pe.wait_ge(s_cut, 1)
            for q in range(4):
                last = te.matmul(cut_psum(q), cut[:, SC * q:SC * q + SC], dst_b[:, 1:EC + 2], start=True, stop=True)
                if q % 2:
                    last.then_inc(s_rows, 1)
            pe.wait_ge(s_pool, 5)
            pe.wait_ge(s_viol, 1)
            te.matmul(ps_b[0:1, 0:1], viols[:], ones[0:EP, 0:1], start=True, stop=True)
            pe.wait_ge(s_pos, 1)
            for q in range(4):
                last = te.matmul(ps_a[0:1, SC * q:SC * q + SC], pos[:, q:q + 1], ident[0:SC, 0:SC], start=True, stop=True)
            last.then_inc(s_posT, 1)

            def transpose_and_sum(i, c):
                s = c % 4
                ps = ps_h[c % 2]
                pe.wait_ge(h_ready, no(i, c) + 1)
                at_least(pe, hT_ready, no(i, c) - 1)
                for j in range(TILES):
                    te.matmul(ps[:, 128 * j:128 * j + 128], h_t[:, c % H_SLOTS, j, :], ident[:], is_transpose=True,
                              start=(j == 0), stop=False, skip_group_check=True)
                pe.wait_ge(sel_ready, no(i, c) + 1)
                pe.wait_ge(lo_ready, no(i, c) + 1)
                for w in range(WINS):
                    o = ps[:, :].rearrange("p (j q) -> p j q", j=TILES)[:, :, WP * w:WP * w + WP]
                    for part in (m_hi, m_lo):
                        last = te.matmul(o, part[:, s, w, :], sel[:, s, w, :, :], start=False,
                                         stop=(w == WINS - 1 and part is m_lo), skip_group_check=True)
                last.then_inc(psh_ready, 1)

            def up(i, c):
                pe.wait_ge(hT_ready, no(i, c) + 1)
                at_least(pe, uT_ready, no(i, c) - 1)
                te.matmul(ps_u[c % 2][:], w1_sb[:], hT[:, c % 4, :], start=True, stop=True).then_inc(psu_ready, 1)

            def down(i, c):
                ps = ps_o[c % 2]
                at_least(pe, o_ready, no(i, c) - 1)
                te.matmul(ps[:], b2_ones[:], b2_rows[:, :, :].rearrange("p j f -> p (j f)"), start=True, stop=False,
                          skip_group_check=True)
                pe.wait_ge(uT_ready, no(i, c) + 1)
                for j in range(TILES):
                    last = te.matmul(ps[:, 128 * j:128 * j + 128], uT[:, c % 4, 128 * j:128 * j + 128], w2_sb[:],
                                     start=False, stop=(j == TILES - 1), skip_group_check=True)
                last.then_inc(pso_ready, 1)

            pe.wait_ge(s_prm, 80)
            pe.wait_ge(s_der, 1)
            pe.wait_ge(s_pool, 7)

            def step(i, c):
                run(transpose_and_sum, i, c, PE_LAG)
                run(up, i, c, UP_LAG)
                run(down, i, c, DOWN_LAG)

            def in_any_order():
                with pe.Fori(0, G_ROUNDS) as t:
                    pe.wait_ge(g_msg, t + 1)
                    te.matmul(ps_a[0:GE, 0:D], g_same, z_t[0:GE, 0, 0, :], start=True, stop=True).then_inc(g_psum, 1)

                def dense(n):
                    pe.wait_ge(g_h, n + 1)
                    for j in range(TILES):
                        last = te.transpose(ps_h[0][:, 128 * j:128 * j + 128], h_t[:, 0, j, :], ident[:])
                    last.then_inc(g_psh, 1)
                    pe.wait_ge(g_hT, n + 1)
                    te.matmul(ps_u[0][:], w1_sb[:], hT[:, 0, :], start=True, stop=True).then_inc(g_psu, 1)
                    pe.wait_ge(g_uT, n + 1)
                    te.matmul(ps_o[0][:], b2_ones[:], b2_rows[:, :, :].rearrange("p j f -> p (j f)"),
                              start=True, stop=False, skip_group_check=True)
                    for j in range(TILES):
                        last = te.matmul(ps_o[0][:, 128 * j:128 * j + 128], uT[:, 0, 128 * j:128 * j + 128], w2_sb[:],
                                         start=False, stop=(j == TILES - 1), skip_group_check=True)
                    last.then_inc(g_pso, 1)

                with pe.Fori(0, LAST) as n:
                    dense(n)
                dense(LAST)

            with pe.If(ordinary(pe) == 0):
                pipeline(pe, step, DOWN_LAG)
            with pe.Else():
                in_any_order()


def kernel(x, src, dst, edge_attr_128, L0_gnn_W1, L0_gnn_b1, L0_gnn_W2, L0_gnn_b2, L0_gnn_eps):
    import numpy as np
    import concourse.bacc as bacc
    from concourse.bass_utils import run_bass_kernel_spmd

    nc = bacc.Bacc("TRN2", target_bir_lowering=False, num_devices=1)
    arrays = {
        "x": np.ascontiguousarray(x),
        "pairs": np.ascontiguousarray(np.stack([np.asarray(src), np.asarray(dst)], axis=1)),
        "dst": np.ascontiguousarray(dst),
        "edge_attr": np.ascontiguousarray(edge_attr_128),
        "w1": np.ascontiguousarray(L0_gnn_W1),
        "b1": np.ascontiguousarray(L0_gnn_b1),
        "w2": np.ascontiguousarray(L0_gnn_W2),
        "b2": np.ascontiguousarray(L0_gnn_b2),
        "eps": np.asarray(L0_gnn_eps).reshape(1),
    }
    args = [nc.dram_tensor("in_" + k, a.shape, mybir.dt.from_np(a.dtype), kind="ExternalInput").ap()
            for k, a in arrays.items()]
    out = nc.dram_tensor("out", (NODES, D), mybir.dt.float32, kind="ExternalOutput").ap()
    gnn_layer(nc, *args, out)
    got = run_bass_kernel_spmd(nc, [{"in_" + k: a for k, a in arrays.items()}], core_ids=[0])
    return got.results[0]["out"]
```

```python
import concourse.bass as bass
from concourse import mybir
from contextlib import ExitStack

NODES = 100000
EDGES = 25000
D = 128
LN_EPS = 1e-5

TILES = 4
BLOCK = 128 * TILES
N_BLOCKS = -(-NODES // BLOCK)
LAST = N_BLOCKS - 1
LAST_BASE = NODES - BLOCK
LAST_P0 = (LAST * BLOCK - LAST_BASE) // TILES
WINS = 2
WNODES = BLOCK // WINS
WP = 128 // WINS
WIN_EDGES = 128
STARTS = N_BLOCKS * WINS
SC = STARTS // 4
MID = 195
assert (NODES - 1) // WNODES - MID < 256 and STARTS - MID <= 256
EP, EC = 125, 200
X_EARLY = 12
EARLY = 12
U = 20
Z_SLOTS = 10
GE = 125
G_ROUNDS = EDGES // GE
ZERO = 10240
ZERO_DMAS = NODES // 125 * D // ZERO
G_STEPS = 10
G_DENSE = 4
BATCH = 4
assert X_EARLY >= EARLY
DVE_EDGES = 8
DVE_EDGES_LAG = 5
B2_BY_DVE = 12
B2_LAG = 10
EARLY_NORM = {"search": ((), (0, 1), (2, 3, 4)), "step": {3: (5, 6, 7, 8), 5: (9, 10), 7: (11,)}}
ATTR_LAG = 4
NORM_LAG = 5
SUM_LAG = 6
HIGH_LAG = 7
LOW_LAG = 8
PE_LAG = 9
COPY_LAG = 10
UP_LAG = 10
RELU_LAG = 11
DOWN_LAG = 12
ADD_LAG = 13
STORE_LAG = 16
EDGE_LAG = 7


def gnn_layer(nc, x, pairs, dst_flat, edge_attr, w1, b1, w2, b2, eps, out):
    fp32 = mybir.dt.float32
    fp32r = mybir.dt.float32r
    bf16 = mybir.dt.bfloat16
    i32 = mybir.dt.int32
    ALU = mybir.AluOpType
    ACT = mybir.ActivationFunctionType
    AX = mybir.AxisListType

    agg = nc.dram_tensor("agg", (NODES, D), fp32).ap()

    ctx = ExitStack()
    with ctx:
        def sb(name, shape, dt):
            return ctx.enter_context(nc.sbuf_tensor(name, shape, dt))

        def pb(name, shape, dt):
            return ctx.enter_context(nc.psum_tensor(name, shape, dt))

        def sem(name):
            return ctx.enter_context(nc.semaphore(name))

        x_t = sb("x_t", [128, U, TILES, D], fp32)
        pair_t = sb("pair_t", [128, U, WINS, 2], i32)
        ea_t = sb("ea_t", [128, U, WINS, D], fp32)
        xs_t = sb("xs_t", [128, U, WINS, D], fp32)
        h_t = sb("h_t", [128, U, TILES, D], fp32)
        z_t = sb("z_t", [128, Z_SLOTS, WINS, D], fp32)
        m_hi = sb("m_hi", [128, 4, WINS, D], fp32r)
        m_lo = sb("m_lo", [128, 4, WINS, D], fp32r)
        sel = sb("sel", [128, 4, WINS, TILES, WP], fp32r)
        rel = sb("rel", [128, U, WINS], fp32)
        hT = sb("hT", [128, 4, BLOCK], fp32)
        uT = sb("uT", [128, 4, BLOCK], fp32)
        o_t = sb("o_t", [128, 4, TILES, D], fp32)
        NS = BATCH * (TILES + WINS)
        stats = sb("stats", [128, U // BATCH, NS, 3], fp32)
        std = sb("std", [128, U // BATCH, NS], fp32)
        rstd = sb("rstd", [128, U // BATCH, NS], fp32)
        nbias = sb("nbias", [128, U // BATCH, NS], fp32)
        ident = sb("ident", [128, 128], fp32)
        ones = sb("ones", [128, 128], fp32)
        w1_sb = sb("w1_sb", [D, D], fp32)
        w2_sb = sb("w2_sb", [D, D], fp32)
        b1_sb = sb("b1_sb", [D, 1], fp32)
        b2_sb = sb("b2_sb", [128, 3, D], fp32)
        b2_part = sb("b2_part", [128, 2, D], bf16)
        b2_rows = sb("b2_rows", [128, TILES, D], bf16)
        b2_ones = sb("b2_ones", [128, 128], bf16)
        eps_sb = sb("eps_sb", [128, 1], fp32)
        opeps = sb("opeps", [128, 1], fp32)
        lneps = sb("lneps", [128, 1], fp32)
        offs = sb("offs", [128, TILES, WP], fp32)
        base = sb("base", [128, U, WINS], fp32)
        dst_i = sb("dst_i", [EP, EC + 1], i32)
        dst_w = sb("dst_w", [EP, EC + 1], i32)
        dst_b = sb("dst_b", [EP, EC + 2], bf16)
        ends = sb("ends", [EP, 2], fp32)
        ends_off = sb("ends_off", [EP, 2], fp32)
        t_row = sb("t_row", [EP, STARTS], bf16)
        t_col = sb("t_col", [SC, 4], fp32)
        below = sb("below", [EP, STARTS], bf16)
        cut = sb("cut", [EP, STARTS], bf16)
        less = sb("less", [SC, 4, EC], fp32)
        cnt = sb("cnt", [SC, 4], fp32)
        pos = sb("pos", [SC, 4], fp32)
        viol = sb("viol", [EP, EC], fp32)
        viols = sb("viols", [EP, 1], fp32)
        row = sb("row", [1, STARTS], fp32)
        gap = sb("gap", [1, STARTS], fp32)
        low = sb("low", [1, 3], fp32)
        starts = sb("starts", [1, STARTS], i32)
        flag = sb("flag", [1, 1], i32)

        ps_h = [pb(f"ps_h{i}", [128, BLOCK], fp32) for i in range(2)]
        ps_u = [pb(f"ps_u{i}", [128, BLOCK], fp32) for i in range(2)]
        ps_o = [pb(f"ps_o{i}", [128, BLOCK], fp32) for i in range(2)]
        ps_a = pb("ps_a", [128, 512], fp32)
        ps_b = pb("ps_b", [128, 512], fp32)

        s_dst = sem("dst_loaded")
        s_eps = sem("eps_loaded")
        s_prm = sem("params_loaded")
        s_pool = sem("pool_constants")
        s_dve = sem("dve_chain")
        pairs_seen = sem("pairs_seen")
        scales_seen = sem("scales_seen")
        s_b2 = sem("b2_split")
        x_seen = sem("x_seen")
        s_der = sem("b2_rows_ready")
        s_cut = sem("cuts_ready")
        s_viol = sem("order_checked")
        s_early = sem("early_stats_done")
        early_std = sem("early_std_ready")
        early_scales_ready = sem("early_scales_ready")
        s_rows = sem("cut_rows_ready")
        s_pos = sem("positions_ready")
        s_posT = sem("positions_row_ready")
        s_flag = sem("starts_and_flag_ready")
        x_loaded = [sem(f"x_loaded{i}") for i in range(U // 2)]
        pair_loaded = [sem(f"pair_loaded{i}") for i in range(U)]
        ea_loaded = [sem(f"ea_loaded{i}") for i in range(U)]
        xs_gathered = [sem(f"xs_gathered{i}") for i in range(U)]
        stored = [sem(f"stored{i}") for i in range(2)]
        stats_ready = sem("stats_ready")
        std_ready = sem("std_ready")
        rstd_ready = sem("rstd_ready")
        scales_ready = sem("scales_ready")
        h_ready = sem("h_ready")
        z_early = sem("z_early")
        z_ready = sem("z_ready")
        v_ready = sem("v_ready")
        hi_ready = sem("hi_ready")
        lo_ready = sem("lo_ready")
        rel_ready = sem("rel_ready")
        base_ready = sem("base_ready")
        sel_ready = sem("sel_ready")
        psh_ready = sem("psh_ready")
        hT_ready = sem("hT_ready")
        psu_ready = sem("psu_ready")
        uT_ready = sem("uT_ready")
        pso_ready = sem("pso_ready")
        xb_ready = sem("xb_ready")
        o_ready = sem("o_ready")

        g_stats = sb("g_stats", [128, TILES, 6], fp32)
        g_mv = sb("g_mv", [128, TILES, 2], fp32)
        g_sd = sb("g_sd", [128, TILES], fp32)
        g_rstd = sb("g_rstd", [128, TILES], fp32)
        g_any_t = sb("g_any_t", [128, 2], fp32)
        g_idx_t = sb("g_idx_t", [128, 1], i32)
        t_idx = sb("t_idx", [128, 1], fp32)
        g_col_t = sb("g_col_t", [128, 128], fp32)
        g_idx, g_any, g_dst = g_idx_t[0:GE, :], g_any_t[0:GE, 0:1], g_any_t[0:GE, 1:2]
        g_col = g_col_t[0:GE, 0:GE]
        g_rows = sb("g_rows", [128, 5, 128], fp32)
        g_row, g_same, g_dup, g_before = (g_rows[0:GE, k, 0:GE] for k in range(4))
        g_row_i = g_rows[0:GE, 4, 0:GE].bitcast(i32)
        agg_flat = agg.rearrange("(p n) f -> p (n f)", p=125)
        zeros = x_t[0:125, :, :, :].rearrange("p u j f -> p (u j f)")[:, 0:ZERO]
        g_zeroed = sem("g_zeroed")
        g_zeros, g_agg, g_in, g_xs, g_dve = (sem("g_" + k) for k in ("zeros", "agg", "in", "xs", "dve"))
        g_var, g_std, g_msg, g_psum, g_sum = (sem("g_" + k) for k in ("var", "std", "msg", "psum", "sum"))
        g_x, g_h, g_psh, g_hT, g_psu, g_uT = (sem("g_" + k) for k in ("x", "h", "psh", "hT", "psu", "uT"))
        g_pso, g_o, g_stored, g_free = (sem("g_" + k) for k in ("pso", "o", "stored", "free"))

        block = ctx.enter_context(nc.Block())

        def cut_psum(q, n=1):
            return ps_h[q // 2][0:SC, q % 2 * (EC + 1):(q % 2 + n) * (EC + 1)]

        def ordinary(eng):
            eng.wait_ge(s_flag, 1)
            return eng.value_load(flag[0:1, 0:1], min_val=0, max_val=3)

        def pipeline(eng, step, lag):
            for c in range(U):
                step(0, c)
            with eng.Fori(1, N_BLOCKS // U) as i:
                for c in range(U):
                    step(i, c)
            for n in range(N_BLOCKS // U * U, N_BLOCKS + lag):
                step(n // U, n % U)

        def run(stage, i, c, lag=0):
            i, c = i + (c - lag) // U, (c - lag) % U
            if not isinstance(i, int) or 0 <= i * U + c < N_BLOCKS:
                stage(i, c)

        def is_last(i, c):
            return isinstance(i, int) and i * U + c == LAST

        def rows_of(batch, first, end):
            return batch.rearrange("p (b r) -> p b r", b=BATCH)[:, :, first:end]

        def b2_by_dve(i, c):
            return isinstance(i, int) and i * U + c >= N_BLOCKS - B2_BY_DVE

        def by_dve(i, c):
            return isinstance(i, int) and i * U + c < DVE_EDGES

        def is_early(i, c):
            return isinstance(i, int) and i * U + c < EARLY

        def no(i, c):
            return i * U + c

        def at_least(eng, sem, value):
            if not isinstance(value, int) or value > 0:
                eng.wait_ge(sem, value)

        def load_x(eng, i, c):
            if isinstance(i, int) and no(i, c) == LAST - 1:
                for b, first in ((0, no(i, c) * BLOCK), (1, LAST_BASE)):
                    eng.dma_start(x_t[:, c + b, :, :], x[first:first + BLOCK, :].rearrange("(p j) f -> p j f", j=TILES)
                                  ).then_inc(x_loaded[c // 2], 16)
            else:
                eng.dma_start(x_t[:, c:c + 2, :, :].rearrange("p b j f -> p b (j f)"),
                              x[bass.ds(no(i, c) * BLOCK, 2 * BLOCK), :].rearrange("(b p j) f -> p b (j f)", b=2, j=TILES)
                              ).then_inc(x_loaded[c // 2], 16)

        @block.sync
        def _(sp):
            dst_rows = dst_flat.rearrange("(p c) -> p c", c=EC)
            nc.sync.dma_start(dst_i[:, 1:EC + 1], dst_rows).then_inc(s_dst, 16)
            sp.wait_ge(s_pool, 1)
            with nc.allow_non_contiguous_dma(reason="124 elements once"):
                nc.sync.dma_start(dst_i[1:EP, 0:1], dst_rows[0:EP - 1, EC - 1:EC]).then_inc(s_dst, 16)

            for c in range(0, X_EARLY, 2):
                load_x(sp, 0, c)

            start_regs = [sp.alloc_register(f"window_start{w}") for w in range(2 * WINS)]

            def load_edges(i, c, tile, source, loaded):
                sp.load(start_regs, starts[0:1, bass.ds(no(i, c) * WINS, 2 * WINS)])
                for b in range(2):
                    for w in range(WINS):
                        s = sp.snap(start_regs[b * WINS + w], min_val=0, max_val=EDGES - WIN_EDGES)
                        sp.dma_start(tile[:, c + b, w, :], source[bass.ds(s, WIN_EDGES), :]).then_inc(loaded[c + b], 16)

            def step(i, c):
                if c % 2 == 0:
                    run(lambda i, c: at_least(sp, v_ready, no(i, c) - U + 2), i, c)
                    run(lambda i, c: load_edges(i, c, pair_t, pairs, pair_loaded), i, c)
                    run(lambda i, c: load_edges(i, c, ea_t, edge_attr, ea_loaded), i, c, ATTR_LAG)

            def in_any_order():
                sp.wait_ge(g_zeros, 1)
                for k in range(ZERO_DMAS):
                    sp.dma_start(agg_flat[:, k * ZERO:k * ZERO + ZERO], zeros).then_inc(g_zeroed, 16)
                sp.wait_ge(g_zeroed, 16 * ZERO_DMAS)

                def load_round(t):
                    rows = bass.ds(t * GE, GE)
                    sp.dma_start(pair_t[0:GE, 0, 0, :], pairs[rows, :]).then_inc(g_in, 16)
                    sp.dma_start(ea_t[0:GE, 0, 0, :], edge_attr[rows, :]).then_inc(g_in, 16)
                    sp.dma_start(g_row_i, dst_flat[rows].rearrange("(o e) -> o e", o=1).to_broadcast([GE, GE])
                                 ).then_inc(g_in, 16)

                load_round(0)
                with sp.Fori(1, G_ROUNDS) as t:
                    sp.wait_ge(g_agg, 16 * t)
                    sp.sem_inc(g_free, 1)
                    load_round(t)
                sp.wait_ge(g_agg, 16 * G_ROUNDS)

                def dense(n):
                    first = LAST_BASE if n is LAST else n * BLOCK
                    p0 = LAST_P0 if n is LAST else 0
                    rows = bass.ds(first, BLOCK)
                    sp.dma_start(x_t[:, 0, :, :], x[rows, :].rearrange("(p j) f -> p j f", j=TILES)).then_inc(g_x, 16)
                    sp.dma_start(x_t[:, 1, :, :], agg[rows, :].rearrange("(p j) f -> p j f", j=TILES)).then_inc(g_x, 16)
                    sp.wait_ge(g_o, n + 1)
                    sp.dma_start(out[bass.ds(n * BLOCK, BLOCK - TILES * p0), :].rearrange("(p j) f -> p (j f)", j=TILES),
                                 o_t[p0:128, 0, :, :].rearrange("p j f -> p (j f)")).then_inc(g_stored, 16)
                    sp.wait_ge(g_stored, 16 * n + 16)
                    sp.sem_inc(g_free, 1)

                with sp.Fori(0, LAST) as n:
                    dense(n)
                dense(LAST)

            with sp.If(ordinary(sp) == 0):
                pipeline(sp, step, ATTR_LAG)
            with sp.Else():
                in_any_order()

        @block.gpsimd
        def _(pool):
            def iota(tile, pattern, first=0, by_partition=0):
                return nc.gpsimd.iota(tile, pattern, base=first, channel_multiplier=by_partition,
                                      allow_small_or_imprecise_dtypes=True)

            nc.gpsimd.memset(dst_i[:, 0:1], -1).then_inc(s_pool, 1)
            iota(t_idx[:], [[0, 1]], by_partition=1)
            nc.gpsimd.memset(ends_off[:], -float(MID)).then_inc(s_pool, 1)
            iota(dst_b[:, EC + 1:EC + 2], [[0, 1]], by_partition=1)
            iota(t_row[:], [[1, STARTS]], first=-MID)
            iota(t_col[:], [[SC, 4]], first=-MID, by_partition=1).then_inc(s_pool, 1)
            nc.gpsimd.memset(lneps[:], LN_EPS)
            nc.gpsimd.memset(ones[:], 1.0).then_inc(s_pool, 1)
            pool.wait_ge(s_pool, 4)
            nc.gpsimd.affine_select(out=ident[:], in_=ones[:], compare_op=ALU.is_equal, fill=0.0, base=0,
                                    pattern=[[-1, 128]], channel_multiplier=1).then_inc(s_pool, 1)
            nc.gpsimd.memset(b2_rows[:], 0.0)
            nc.gpsimd.memset(b2_ones[:], 1.0).then_inc(s_pool, 1)
            iota(base[:], [[WNODES, U * WINS]])
            iota(offs[:], [[1, TILES], [TILES, WP]])
            iota(g_col_t[:], [[1, 128]]).then_inc(s_pool, 1)

            def gather(i, c):
                pool.wait_ge(pair_loaded[c], 16 * WINS * (i + 1))
                pool.sem_inc(pairs_seen, 1)
                for w in range(WINS):
                    pool.indirect_dma_start(
                        out=xs_t[:, c, w, :], out_offset=None, in_=x,
                        in_offset=bass.IndirectOffsetOnAxis(ap=pair_t[:, c, w, 0:1], axis=0),
                    ).then_inc(xs_gathered[c], 16)

            def normalise_edges(i, c):
                k = c // BATCH
                at_least(pool, lo_ready, no(i, c) - Z_SLOTS + 1)
                pool.wait_ge(scales_ready, i * (U // BATCH) + k + 1)
                pool.sem_inc(scales_seen, 1)
                for w in range(WINS):
                    q = c % BATCH * (TILES + WINS) + TILES + w
                    last = nc.gpsimd.tensor_scalar(z_t[:, c % Z_SLOTS, w, :], xs_t[:, c, w, :], rstd[:, k, q:q + 1],
                                                   nbias[:, k, q:q + 1], ALU.mult, ALU.add)
                last.then_inc(z_ready, 1)

            def step(i, c):
                run(gather, i, c)
                if not by_dve(i, c - EDGE_LAG):
                    run(normalise_edges, i, c, EDGE_LAG)

            def in_any_order():
                with pool.Fori(0, G_ROUNDS) as t:
                    pool.wait_ge(g_in, 48 * t + 48)
                    pool.sem_inc(pairs_seen, 1)
                    pool.indirect_dma_start(
                        out=xs_t[0:GE, 0, 0, :], out_offset=None, in_=x,
                        in_offset=bass.IndirectOffsetOnAxis(ap=pair_t[0:GE, 0, 0, 0:1], axis=0)).then_inc(g_xs, 16)
                    pool.indirect_dma_start(
                        out=xs_t[0:GE, 0, 1, :], out_offset=None, in_=agg,
                        in_offset=bass.IndirectOffsetOnAxis(ap=pair_t[0:GE, 0, 0, 1:2], axis=0)).then_inc(g_xs, 16)
                    pool.wait_ge(g_sum, t + 1)
                    pool.sem_inc(scales_seen, 1)
                    pool.indirect_dma_start(
                        out=agg, out_offset=bass.IndirectOffsetOnAxis(ap=g_idx, axis=0), in_=xs_t[0:GE, 0, 1, :],
                        in_offset=None, bounds_check=NODES - 1, oob_is_err=False).then_inc(g_agg, 16)

            with pool.If(ordinary(pool) == 0):
                pipeline(pool, step, EDGE_LAG)
            with pool.Else():
                in_any_order()

        @block.vector
        def _(dve):
            ve = nc.vector
            chain = [0]

            def link(ins):
                chain[0] += 1
                ins.then_inc(s_dve, 1)
                dve.wait_ge(s_dve, chain[0])

            def node_stats(i, c):
                k = c // BATCH
                o = (c % BATCH) * (TILES + WINS)
                dve.wait_ge(x_loaded[c // 2], 16 * (i + (2 if isinstance(i, int) and no(i, c) >= LAST - 1 else 1)))
                for j in range(0, TILES, 2):
                    last = ve.bn_stats(stats[:, k, o + j:o + j + 2, :].rearrange("p a b -> p (a b)"),
                                       x_t[:, c, j:j + 2, :].rearrange("p j f -> p f j"))
                return last

            def early_scales(k):
                sd, rs, nb = (rows_of(t[:, k, :], 0, TILES) for t in (std, rstd, nbias))
                dve.wait_ge(early_std, k + 1)
                link(ve.reciprocal(rs, sd))
                link(ve.tensor_scalar(rs, rs, opeps[:], None, ALU.mult))
                ve.scalar_tensor_tensor(out=nb, in0=rows_of(stats[:, k, :, 1], 0, TILES), scalar=-1.0, in1=rs,
                                        op0=ALU.mult, op1=ALU.mult).then_inc(early_scales_ready, 1)

            dve.wait_ge(s_pool, 2)
            link(ve.tensor_scalar(viols[:], t_idx[0:EP, :], EP - 1.5, float(2 * STARTS), ALU.is_gt, ALU.mult))
            link(ve.tensor_tensor(ends_off[:, 1:2], ends_off[:, 1:2], viols[:], ALU.add))
            dve.wait_ge(s_dst, 32)
            link(ve.tensor_scalar(dst_w[:], dst_i[:], WNODES.bit_length() - 1, None, ALU.arith_shift_right))
            ve.tensor_tensor(ends[:], dst_w[:, 0:EC + 1:EC], ends_off[:], ALU.add)
            dve.wait_ge(s_pool, 3)
            link(ve.tensor_scalar(dst_b[:, 0:EC + 1], dst_w[:], -float(MID), None, ALU.add))
            ve.tensor_scalar(below[:], t_row[:], ends[:, 1:2], None, ALU.is_gt)
            link(ve.tensor_scalar(cut[:], t_row[:], ends[:, 0:1], None, ALU.is_gt))
            ve.tensor_tensor(cut[:], cut[:], below[:], ALU.subtract).then_inc(s_cut, 1)
            link(ve.tensor_tensor(viol[:], dst_i[:, 1:EC + 1], dst_i[:, 0:EC], ALU.is_lt))
            ve.tensor_reduce(viols[:], viol[:], AX.X, ALU.add).then_inc(s_viol, 1)
            dve.wait_ge(s_eps, 16)
            link(ve.tensor_scalar(opeps[:], eps_sb[:], 1.0, None, ALU.add))
            ve.tensor_scalar(low[:, 2:3], opeps[0:1, :], 0.0, None, ALU.is_lt)
            for q in (0, 2):
                dve.wait_ge(s_rows, q // 2 + 1)
                last = ve.tensor_tensor(less[:, q:q + 2, :], cut_psum(q, 2).rearrange("p (q e) -> p q e", q=2)[:, :, 0:EC],
                                        t_col[:, q:q + 2].unsqueeze(2).broadcast_to([SC, 2, EC]), ALU.is_lt)
            link(last)
            link(ve.tensor_reduce(cnt[:], less[:], AX.X, ALU.add))
            for q in (0, 2):
                last = ve.scalar_tensor_tensor(out=pos[:, q:q + 2], scalar=float(EC), in1=cnt[:, q:q + 2],
                                               in0=cut_psum(q, 2).rearrange("p (q e) -> p q e", q=2)[:, :, EC],
                                               op0=ALU.mult, op1=ALU.add)
            last.then_inc(s_pos, 1)
            dve.wait_ge(s_posT, 1)
            link(ve.tensor_copy(row[:], ps_a[0:1, 0:STARTS]))
            ve.tensor_tensor(gap[:, 0:STARTS - 1], row[:, 1:STARTS], row[:, 0:STARTS - 1], ALU.subtract)
            link(ve.scalar_tensor_tensor(out=low[:, 1:2], in0=ps_b[0:1, 0:1], scalar=0.5, in1=low[:, 2:3],
                                         op0=ALU.is_gt, op1=ALU.add))
            link(ve.tensor_reduce(low[:, 0:1], gap[:, 0:STARTS - 1], AX.X, ALU.max))
            ve.tensor_scalar(starts[:], row[:], float(EDGES - WIN_EDGES), None, ALU.min)
            ve.scalar_tensor_tensor(out=flag[:], in0=low[:, 0:1], scalar=WIN_EDGES + 0.5, in1=low[:, 1:2],
                                    op0=ALU.is_gt, op1=ALU.add).then_inc(s_flag, 1)
            dve.wait_ge(s_prm, 64)
            link(ve.tensor_copy(b2_part[:, 0, :], b2_sb[:, 0, :]))
            link(ve.tensor_tensor(b2_sb[:, 1, :], b2_sb[:, 0, :], b2_part[:, 0, :], ALU.subtract))
            link(ve.tensor_copy(b2_part[:, 1, :], b2_sb[:, 1, :]))
            ve.tensor_tensor(b2_sb[:, 2, :], b2_sb[:, 1, :], b2_part[:, 1, :], ALU.subtract).then_inc(s_b2, 1)
            for k in range(EARLY // BATCH):
                for c in range(k * BATCH, (k + 1) * BATCH):
                    last = node_stats(0, c)
                last.then_inc(s_early, 1)
                if k > 0:
                    early_scales(k - 1)
            early_scales(EARLY // BATCH - 1)

            def rows_stats(i, c):
                k = c // BATCH
                o = (c % BATCH) * (TILES + WINS)
                if not is_early(i, c):
                    node_stats(i, c)
                dve.wait_ge(xs_gathered[c], 16 * WINS * (i + 1))
                last = ve.bn_stats(stats[:, k, o + TILES:o + TILES + WINS, :].rearrange("p a b -> p (a b)"),
                                   xs_t[:, c, :, :].rearrange("p j f -> p f j"))
                if c % BATCH == BATCH - 1:
                    last.then_inc(stats_ready, 1)

            def batch_no(i, c):
                return i * (U // BATCH) + c // BATCH + 1

            def rows_left(i, c, tile):
                return rows_of(tile[:, c // BATCH, :], TILES, TILES + WINS) if is_early(i, c) else tile[:, c // BATCH, :]

            def reciprocals(i, c):
                dve.wait_ge(std_ready, batch_no(i, c))
                ve.reciprocal(rows_left(i, c, rstd), rows_left(i, c, std)).then_inc(rstd_ready, 2 if is_early(i, c) else 1)

            def node_factor(i, c):
                if not is_early(i, c):
                    dve.wait_ge(rstd_ready, 2 * batch_no(i, c) - 1)
                    rn = rows_of(rstd[:, c // BATCH, :], 0, TILES)
                    ve.tensor_scalar(rn, rn, opeps[:], None, ALU.mult).then_inc(rstd_ready, 1)

            def offsets(i, c):
                dve.wait_ge(rstd_ready, 2 * batch_no(i, c))
                ve.scalar_tensor_tensor(out=rows_left(i, c, nbias), in0=rows_left(i, c, stats[:, :, :, 1]), scalar=-1.0,
                                        in1=rows_left(i, c, rstd), op0=ALU.mult, op1=ALU.mult).then_inc(scales_ready, 1)

            def early_edges(i, c):
                k = c // BATCH
                dve.wait_ge(scales_ready, batch_no(i, c))
                at_least(dve, lo_ready, no(i, c) - Z_SLOTS + 1)
                for w in range(WINS):
                    q = c % BATCH * (TILES + WINS) + TILES + w
                    last = ve.tensor_scalar(z_t[:, c % Z_SLOTS, w, :], xs_t[:, c, w, :], rstd[:, k, q:q + 1],
                                            nbias[:, k, q:q + 1], ALU.mult, ALU.add)
                last.then_inc(z_early, 1)

            def edge_sum(i, c):
                if by_dve(i, c):
                    dve.wait_ge(z_early, no(i, c) + 1)
                else:
                    dve.wait_ge(z_ready, no(i, c) + 1 - DVE_EDGES)
                dve.wait_ge(ea_loaded[c], 16 * WINS * (i + 1))
                ve.scalar_tensor_tensor(out=z_t[:, c % Z_SLOTS, :, :], in0=z_t[:, c % Z_SLOTS, :, :], scalar=0.0, in1=ea_t[:, c, :, :],
                                        op0=ALU.max, op1=ALU.add).then_inc(v_ready, 1)

            def edge_low(i, c):
                s = c % 4
                dve.wait_ge(hi_ready, no(i, c) + 1)
                ve.scalar_tensor_tensor(out=m_lo[:, s, :, :], in0=z_t[:, c % Z_SLOTS, :, :], scalar=0.0,
                                        in1=m_hi[:, s, :, :].bitcast(fp32),
                                        op0=ALU.max, op1=ALU.subtract).then_inc(lo_ready, 1)

            def move_base(i, c):
                if c == BATCH - 1 and not (isinstance(i, int) and i == 0):
                    dve.wait_ge(rel_ready, i * (U // BATCH))
                    ve.tensor_scalar(base[:], base[:], float(U * BLOCK), None, ALU.add).then_inc(base_ready, 1)

            def relative(i, c):
                if c == BATCH - 1 and not (isinstance(i, int) and i == 0):
                    dve.wait_ge(base_ready, i)
                first = c - BATCH + 1
                end = c if is_last(i, c) else c + 1
                last = ve.tensor_tensor(rel[:, first:end, :], pair_t[:, first:end, :, 1], base[:, first:end, :],
                                        ALU.subtract)
                if is_last(i, c):
                    for w in range(WINS):
                        last = ve.tensor_scalar(rel[:, c, w:w + 1], pair_t[:, c, w, 1:2],
                                                -float(LAST_BASE + w * WNODES), None, ALU.add)
                last.then_inc(rel_ready, 1)

            def select(i, c):
                s = c % 4
                dve.wait_ge(rel_ready, i * (U // BATCH) + c // BATCH + 1)
                at_least(dve, psh_ready, no(i, c) - 3)
                for w in range(WINS):
                    last = ve.tensor_scalar(sel[:, s, w, :, :], offs[:], rel[:, c, w:w + 1], None, ALU.is_equal)
                last.then_inc(sel_ready, 1)

            def add_b2(i, c):
                dve.wait_ge(h_ready, no(i, c) + 1)
                ve.tensor_tensor(x_t[:, c, :, :], x_t[:, c, :, :],
                                 b2_sb[:, 0, :].unsqueeze(1).broadcast_to([128, TILES, D]), ALU.add).then_inc(xb_ready, 1)

            def add(i, c):
                s = c % 4
                dve.wait_ge(pso_ready, no(i, c) + 1)
                at_least(dve, stored[s // 2], 16 * (i * (U // 4) + c // 4))
                if b2_by_dve(i, c):
                    dve.wait_ge(xb_ready, no(i, c) + 1 - (N_BLOCKS - B2_BY_DVE))
                ve.tensor_tensor(o_t[:, s, :, :].rearrange("p j f -> p (j f)"), ps_o[c % 2][:],
                                 x_t[:, c, :, :].rearrange("p j f -> p (j f)"), ALU.add).then_inc(o_ready, 1)

            def step(i, c):
                run(rows_stats, i, c)
                run(add, i, c, ADD_LAG)
                batch_ended = c % BATCH == 0
                if batch_ended:
                    run(move_base, i, c, 1)
                    run(reciprocals, i, c, 1)
                if b2_by_dve(i, c - B2_LAG):
                    run(add_b2, i, c, B2_LAG)
                run(select, i, c, LOW_LAG)
                if batch_ended:
                    run(node_factor, i, c, 1)
                run(edge_low, i, c, LOW_LAG)
                if batch_ended:
                    run(offsets, i, c, 1)
                run(edge_sum, i, c, SUM_LAG)
                if isinstance(i, int) and by_dve(i, c - DVE_EDGES_LAG):
                    run(early_edges, i, c, DVE_EDGES_LAG)
                if batch_ended:
                    run(relative, i, c, 1)

            def in_any_order():
                dve.wait_ge(s_early, EARLY // BATCH)
                dve.wait_ge(h_ready, sum(len(blocks) for blocks in EARLY_NORM["search"]))
                for k in range(X_EARLY // 2):
                    dve.wait_ge(x_loaded[k], 16)
                    dve.sem_inc(x_seen, 1)
                ve.memset(zeros, 0.0).then_inc(g_zeros, 1)
                ve.tensor_scalar(g_before, g_col, t_idx[0:GE, :], None, ALU.is_lt)

                with dve.Fori(0, G_ROUNDS) as t:
                    step_no = [0]

                    def then(ins):
                        step_no[0] += 1
                        ins.then_inc(g_dve, 1)
                        dve.wait_ge(g_dve, t * G_STEPS + step_no[0])

                    xs, ag, msg = xs_t[0:GE, 0, 0, :], xs_t[0:GE, 0, 1, :], z_t[0:GE, 0, 0, :]
                    st, mv = g_stats[0:GE, 0, :], g_mv[0:GE, 0, :]
                    dve.wait_ge(g_xs, 32 * t + 32)
                    then(ve.bn_stats(st, xs))
                    ve.tensor_copy(g_dst, pair_t[0:GE, 0, 0, 1:2])
                    ve.bn_aggr(mv, st).then_inc(g_var, 1)
                    dve.wait_ge(g_std, t + 1)
                    then(ve.reciprocal(g_rstd[0:GE, 0:1], g_sd[0:GE, 0:1]))
                    then(ve.tensor_scalar(msg, xs, mv[:, 0:1], g_rstd[0:GE, 0:1], ALU.subtract, ALU.mult))
                    then(ve.scalar_tensor_tensor(out=msg, in0=msg, scalar=0.0, in1=ea_t[0:GE, 0, 0, :],
                                                 op0=ALU.max, op1=ALU.add))
                    then(ve.tensor_scalar(msg, msg, 0.0, None, ALU.max))
                    then(ve.tensor_copy(g_row, g_row_i))
                    ve.tensor_scalar(g_same, g_row, g_dst, None, ALU.is_equal).then_inc(g_msg, 1)
                    dve.wait_ge(g_msg, t + 1)
                    then(ve.tensor_tensor(g_dup, g_same, g_before, ALU.mult))
                    then(ve.tensor_reduce(g_any, g_dup, AX.X, ALU.max))
                    then(ve.tensor_scalar(g_any, g_any, float(1 << 20), None, ALU.mult))
                    then(ve.tensor_tensor(g_idx, g_any, g_dst, ALU.add))
                    dve.wait_ge(g_psum, t + 1)
                    ve.tensor_tensor(ag, ps_a[0:GE, 0:D], ag, ALU.add).then_inc(g_sum, 1)
                    assert step_no[0] == G_STEPS

                def dense(n):
                    step_no = [0]

                    def then(ins):
                        step_no[0] += 1
                        ins.then_inc(g_dve, 1)
                        dve.wait_ge(g_dve, G_ROUNDS * G_STEPS + n * G_DENSE + step_no[0])

                    dve.wait_ge(g_x, 32 * n + 32)
                    for j in range(TILES):
                        last = ve.bn_stats(g_stats[:, j, :], x_t[:, 0, j, :])
                    then(last)
                    ve.tensor_copy(g_any_t[:, 0:1], t_idx[:])
                    for j in range(TILES):
                        last = ve.bn_aggr(g_mv[:, j, :], g_stats[:, j, :])
                    last.then_inc(g_var, 1)
                    dve.wait_ge(g_std, G_ROUNDS + n + 1)
                    then(ve.reciprocal(g_rstd[:], g_sd[:]))
                    for j in range(TILES):
                        last = ve.tensor_scalar(h_t[:, 0, j, :], x_t[:, 0, j, :], g_mv[:, j, 0:1], g_rstd[:, j:j + 1],
                                                ALU.subtract, ALU.mult)
                    then(last)
                    then(ve.tensor_scalar(h_t[:, 0, :, :], h_t[:, 0, :, :], 0.0, opeps[:], ALU.max, ALU.mult))
                    ve.tensor_tensor(h_t[:, 0, :, :], h_t[:, 0, :, :], x_t[:, 1, :, :], ALU.add).then_inc(g_h, 1)
                    dve.wait_ge(g_pso, n + 1)
                    ve.tensor_tensor(o_t[:, 0, :, :].rearrange("p j f -> p (j f)"), ps_o[0][:],
                                     x_t[:, 0, :, :].rearrange("p j f -> p (j f)"), ALU.add).then_inc(g_o, 1)
                    assert step_no[0] == G_DENSE

                with dve.Fori(0, LAST) as n:
                    dense(n)
                dense(LAST)

            dve.wait_ge(s_pool, 7)
            with dve.If(ordinary(dve) == 0):
                pipeline(dve, step, ADD_LAG)
            with dve.Else():
                in_any_order()

        @block.scalar
        def _(act):
            sc = nc.scalar

            def store(i, c):
                k = c % 4 // 2
                act.wait_ge(o_ready, no(i, c) + 2)
                if isinstance(i, int) and no(i, c) == LAST - 1:
                    act.dma_start(out[(LAST - 1) * BLOCK:LAST * BLOCK, :].rearrange("(p j) f -> p (j f)", j=TILES),
                                  o_t[:, 2 * k, :, :].rearrange("p j f -> p (j f)")).then_inc(stored[k], 16)
                    act.dma_start(out[LAST * BLOCK:NODES, :].rearrange("(p j) f -> p (j f)", j=TILES),
                                  o_t[LAST_P0:128, 2 * k + 1, :, :].rearrange("p j f -> p (j f)")).then_inc(stored[k], 16)
                else:
                    act.dma_start(out[bass.ds(no(i, c) * BLOCK, 2 * BLOCK), :].rearrange("(b p j) f -> p b (j f)", b=2, j=TILES),
                                  o_t[:, 2 * k:2 * k + 2, :, :].rearrange("p b j f -> p b (j f)")).then_inc(stored[k], 16)

            def deviations(i, c):
                k = c // BATCH
                act.wait_ge(stats_ready, i * (U // BATCH) + k + 1)
                sd, squares = std[:, k, :], stats[:, k, :, 2]
                if is_early(i, c):
                    sd, squares = (rows_of(t, TILES, TILES + WINS) for t in (sd, squares))
                sc.activation(sd, squares, ACT.Sqrt, bias=lneps[:], scale=1.0 / D).then_inc(std_ready, 1)

            def normalise(i, c):
                k = c // BATCH
                o = (c % BATCH) * (TILES + WINS)
                if is_early(i, c):
                    act.wait_ge(early_scales_ready, k + 1)
                else:
                    act.wait_ge(scales_ready, i * (U // BATCH) + k + 1)
                for j in range(TILES):
                    last = sc.activation(h_t[:, c, j, :], x_t[:, c, j, :], ACT.Relu,
                                         bias=nbias[:, k, o + j:o + j + 1], scale=rstd[:, k, o + j:o + j + 1])
                last.then_inc(h_ready, 1)

            def edge_high(i, c):
                s = c % 4
                act.wait_ge(v_ready, no(i, c) + 1)
                at_least(act, psh_ready, no(i, c) - 3)
                sc.activation(m_hi[:, s, :, :], z_t[:, c % Z_SLOTS, :, :], ACT.Relu).then_inc(hi_ready, 1)

            def copy_h(i, c):
                act.wait_ge(psh_ready, no(i, c) + 1)
                at_least(act, psu_ready, no(i, c) - 3)
                sc.activation(hT[:, c % 4, :], ps_h[c % 2][:], ACT.Copy).then_inc(hT_ready, 1)

            def bias_relu(i, c):
                act.wait_ge(psu_ready, no(i, c) + 1)
                at_least(act, pso_ready, no(i, c) - 3)
                sc.activation(uT[:, c % 4, :], ps_u[c % 2][:], ACT.Relu, bias=b1_sb[:]).then_inc(uT_ready, 1)

            with nc.allow_non_contiguous_dma(reason="129 elements once"):
                act.dma_start(eps_sb[:], eps.rearrange("(o f) -> o f", o=1).to_broadcast([128, 1])).then_inc(s_eps, 16)
                act.dma_start(b1_sb[:], b1.rearrange("(p o) -> p o", o=1)).then_inc(s_prm, 16)
            act.dma_start(b2_sb[:, 0, :], b2.rearrange("(o f) -> o f", o=1).to_broadcast([128, D])).then_inc(s_prm, 16)
            act.dma_start(w1_sb[:], w1).then_inc(s_prm, 16)
            act.dma_start(w2_sb[:], w2).then_inc(s_prm, 16)
            act.wait_ge(s_pool, 6)
            for k in range(EARLY // BATCH):
                act.wait_ge(s_early, k + 1)
                sc.activation(rows_of(std[:, k, :], 0, TILES), rows_of(stats[:, k, :, 2], 0, TILES), ACT.Sqrt,
                              bias=lneps[:], scale=1.0 / D).then_inc(early_std, 1)
                for c in EARLY_NORM["search"][k]:
                    normalise(0, c)
            act.wait_ge(s_prm, 64)
            act.wait_ge(s_b2, 1)
            for r, part in ((0, 0), (32, 1), (64, 2)):
                last = sc.activation(b2_rows[r:r + 1, :, :], b2_sb[r:r + 1, part, :].unsqueeze(1).broadcast_to([1, TILES, D]),
                                     ACT.Copy)
            last.then_inc(s_der, 1)

            def step(i, c):
                if isinstance(i, int) and i == 0 and c % 2 == 0 and X_EARLY + c < U:
                    load_x(act, 0, X_EARLY + c)
                if (c - STORE_LAG) % 2 == 0:
                    run(store, i, c, STORE_LAG)
                    if not (isinstance(i, int) and i * U + c < STORE_LAG):
                        run(lambda i, c: load_x(act, i, c), i, c, STORE_LAG - U)
                run(copy_h, i, c, COPY_LAG)
                if c % BATCH == BATCH - 1:
                    run(deviations, i, c)
                if isinstance(i, int) and i == 0:
                    for k in EARLY_NORM["step"].get(c, ()):
                        normalise(0, k)
                if not is_early(i, c - NORM_LAG):
                    run(normalise, i, c, NORM_LAG)
                run(bias_relu, i, c, RELU_LAG)
                run(edge_high, i, c, HIGH_LAG)

            def in_any_order():
                with act.Fori(0, G_ROUNDS) as t:
                    act.wait_ge(g_var, t + 1)
                    sc.activation(g_sd[0:GE, 0:1], g_mv[0:GE, 0, 1:2], ACT.Sqrt, bias=lneps[0:GE, :]).then_inc(g_std, 1)

                def dense(n):
                    act.wait_ge(g_var, G_ROUNDS + n + 1)
                    sc.activation(g_sd[:], g_mv[:, :, 1], ACT.Sqrt, bias=lneps[:]).then_inc(g_std, 1)
                    act.wait_ge(g_psh, n + 1)
                    sc.activation(hT[:, 0, :], ps_h[0][:], ACT.Copy).then_inc(g_hT, 1)
                    act.wait_ge(g_psu, n + 1)
                    sc.activation(uT[:, 0, :], ps_u[0][:], ACT.Relu, bias=b1_sb[:]).then_inc(g_uT, 1)

                with act.Fori(0, LAST) as n:
                    dense(n)
                dense(LAST)

            with act.If(ordinary(act) == 0):
                pipeline(act, step, STORE_LAG)
                act.wait_ge(stored[0], 16 * (N_BLOCKS // 4))
                act.wait_ge(stored[1], 16 * (N_BLOCKS // 4 + 1))
            with act.Else():
                in_any_order()

        @block.tensor
        def _(pe):
            te = nc.tensor
            pe.wait_ge(s_cut, 1)
            for q in range(4):
                last = te.matmul(cut_psum(q), cut[:, SC * q:SC * q + SC], dst_b[:, 1:EC + 2], start=True, stop=True)
                if q % 2:
                    last.then_inc(s_rows, 1)
            pe.wait_ge(s_pool, 5)
            pe.wait_ge(s_viol, 1)
            te.matmul(ps_b[0:1, 0:1], viols[:], ones[0:EP, 0:1], start=True, stop=True)
            pe.wait_ge(s_pos, 1)
            for q in range(4):
                last = te.matmul(ps_a[0:1, SC * q:SC * q + SC], pos[:, q:q + 1], ident[0:SC, 0:SC], start=True, stop=True)
            last.then_inc(s_posT, 1)

            def transpose_and_sum(i, c):
                s = c % 4
                ps = ps_h[c % 2]
                pe.wait_ge(h_ready, no(i, c) + 1)
                at_least(pe, hT_ready, no(i, c) - 1)
                for j in range(TILES):
                    te.matmul(ps[:, 128 * j:128 * j + 128], h_t[:, c, j, :], ident[:], is_transpose=True,
                              start=(j == 0), stop=False, skip_group_check=True)
                pe.wait_ge(sel_ready, no(i, c) + 1)
                pe.wait_ge(lo_ready, no(i, c) + 1)
                for w in range(WINS):
                    o = ps[:, :].rearrange("p (j q) -> p j q", j=TILES)[:, :, WP * w:WP * w + WP]
                    for part in (m_hi, m_lo):
                        last = te.matmul(o, part[:, s, w, :], sel[:, s, w, :, :], start=False,
                                         stop=(w == WINS - 1 and part is m_lo), skip_group_check=True)
                last.then_inc(psh_ready, 1)

            def up(i, c):
                pe.wait_ge(hT_ready, no(i, c) + 1)
                at_least(pe, uT_ready, no(i, c) - 1)
                te.matmul(ps_u[c % 2][:], w1_sb[:], hT[:, c % 4, :], start=True, stop=True).then_inc(psu_ready, 1)

            def down(i, c):
                ps = ps_o[c % 2]
                at_least(pe, o_ready, no(i, c) - 1)
                with_b2 = not b2_by_dve(i, c)
                if with_b2:
                    te.matmul(ps[:], b2_ones[:], b2_rows[:, :, :].rearrange("p j f -> p (j f)"), start=True, stop=False,
                              skip_group_check=True)
                pe.wait_ge(uT_ready, no(i, c) + 1)
                for j in range(TILES):
                    last = te.matmul(ps[:, 128 * j:128 * j + 128], uT[:, c % 4, 128 * j:128 * j + 128], w2_sb[:],
                                     start=(j == 0 and not with_b2), stop=(j == TILES - 1), skip_group_check=True)
                last.then_inc(pso_ready, 1)

            pe.wait_ge(s_prm, 64)
            pe.wait_ge(s_der, 1)
            pe.wait_ge(s_pool, 7)

            def step(i, c):
                run(transpose_and_sum, i, c, PE_LAG)
                run(up, i, c, UP_LAG)
                run(down, i, c, DOWN_LAG)

            def in_any_order():
                with pe.Fori(0, G_ROUNDS) as t:
                    pe.wait_ge(g_msg, t + 1)
                    te.matmul(ps_a[0:GE, 0:D], g_same, z_t[0:GE, 0, 0, :], start=True, stop=True).then_inc(g_psum, 1)

                def dense(n):
                    pe.wait_ge(g_h, n + 1)
                    for j in range(TILES):
                        last = te.transpose(ps_h[0][:, 128 * j:128 * j + 128], h_t[:, 0, j, :], ident[:])
                    last.then_inc(g_psh, 1)
                    pe.wait_ge(g_hT, n + 1)
                    te.matmul(ps_u[0][:], w1_sb[:], hT[:, 0, :], start=True, stop=True).then_inc(g_psu, 1)
                    pe.wait_ge(g_uT, n + 1)
                    te.matmul(ps_o[0][:], b2_ones[:], b2_rows[:, :, :].rearrange("p j f -> p (j f)"),
                              start=True, stop=False, skip_group_check=True)
                    for j in range(TILES):
                        last = te.matmul(ps_o[0][:, 128 * j:128 * j + 128], uT[:, 0, 128 * j:128 * j + 128], w2_sb[:],
                                         start=False, stop=(j == TILES - 1), skip_group_check=True)
                    last.then_inc(g_pso, 1)

                with pe.Fori(0, LAST) as n:
                    dense(n)
                dense(LAST)

            with pe.If(ordinary(pe) == 0):
                pipeline(pe, step, DOWN_LAG)
            with pe.Else():
                in_any_order()


def kernel(x, src, dst, edge_attr_128, L0_gnn_W1, L0_gnn_b1, L0_gnn_W2, L0_gnn_b2, L0_gnn_eps):
    import numpy as np
    import concourse.bacc as bacc
    from concourse.bass_utils import run_bass_kernel_spmd

    nc = bacc.Bacc("TRN2", target_bir_lowering=False, num_devices=1)
    arrays = {
        "x": np.ascontiguousarray(x),
        "pairs": np.ascontiguousarray(np.stack([np.asarray(src), np.asarray(dst)], axis=1)),
        "dst": np.ascontiguousarray(dst),
        "edge_attr": np.ascontiguousarray(edge_attr_128),
        "w1": np.ascontiguousarray(L0_gnn_W1),
        "b1": np.ascontiguousarray(L0_gnn_b1),
        "w2": np.ascontiguousarray(L0_gnn_W2),
        "b2": np.ascontiguousarray(L0_gnn_b2),
        "eps": np.asarray(L0_gnn_eps).reshape(1),
    }
    args = [nc.dram_tensor("in_" + k, a.shape, mybir.dt.from_np(a.dtype), kind="ExternalInput").ap()
            for k, a in arrays.items()]
    out = nc.dram_tensor("out", (NODES, D), mybir.dt.float32, kind="ExternalOutput").ap()
    gnn_layer(nc, *args, out)
    got = run_bass_kernel_spmd(nc, [{"in_" + k: a for k, a in arrays.items()}], core_ids=[0])
    return got.results[0]["out"]
```
